# Optimizing a Trainium2 kernel written in Bass

```python
import numpy as np
import jax
import jax.numpy as jnp

def _softmax(x, axis=-1):
    return jax.nn.softmax(x, axis=axis)

def _gelu(x):
    return jax.nn.gelu(x, approximate=True)

def _silu(x):
    return jax.nn.silu(x)

def _sigmoid(x):
    return jax.nn.sigmoid(x)

def _layernorm(x, axis=-1, eps=1e-05):
    m = jnp.mean(x, axis=axis, keepdims=True)
    v = jnp.var(x, axis=axis, keepdims=True)
    return (x - m) / jnp.sqrt(v + eps)

def _scatter_add(tgt, idx, src, axis=0):
    return tgt.at[idx].add(src)

def _segment_sum(src, seg, n):
    return jax.ops.segment_sum(src, seg, n)
kernel_name = 'mk_cond_resid_d2_seqx_r4_c43050'

def setup_inputs(seed: int=0):
    np.random.seed(seed)
    _w = jnp.asarray

    def _rec_inputs():
        import jax
        import jax.numpy as jnp
        _rk = jax.random.key(seed)
        x = -0.000125 + 0.9999 * jax.random.normal(jax.random.fold_in(_rk, 1), (64, 64, 256), jnp.float32)
        _lenS = 64 - jax.random.randint(jax.random.fold_in(_rk, 7), (64,), 0, max(1, 64 // 4) + 1, jnp.int32)
        _lenS2 = 64 - jax.random.randint(jax.random.fold_in(_rk, 8), (64,), 0, max(1, 64 // 4) + 1, jnp.int32)
        cond_1024 = 0.00782532 + 1.00527 * jax.random.normal(jax.random.fold_in(_rk, 11), (64, 256), jnp.float32)
        return (x, cond_1024)
    x, cond_1024 = _rec_inputs()

    def _L0_cond_setup():
        import jax, jax.numpy as jnp
        import numpy as np
        B, S, D = (8, 1024, 256)
        H = 16
        HD = D // H
        ACT_DIM = 256
        key = jax.random.key(seed)
        ks = jax.random.split(key, 10)
        s = 0.02
        return {'hidden_states': jax.random.normal(ks[0], (B, S, D), jnp.float32), 'activation': jax.random.normal(ks[1], (B, ACT_DIM), jnp.float32), 'W_q': jax.random.normal(ks[2], (D, D), jnp.float32) * s, 'b_q': jnp.zeros((D,), jnp.float32), 'W_kv': jax.random.normal(ks[3], (ACT_DIM, 2 * D), jnp.float32) * s, 'b_kv': jnp.zeros((2 * D,), jnp.float32), 'no_op_k': jax.random.normal(ks[4], (1, H, 1, HD), jnp.float32) * s, 'no_op_v': jax.random.normal(ks[5], (1, H, 1, HD), jnp.float32) * s, 'W_proj': jax.random.normal(ks[6], (D, D), jnp.float32) * s, 'b_proj': jnp.zeros((D,), jnp.float32)}
    _L0_cond_all = _L0_cond_setup()
    _L0_cond_in = {k: v for k, v in _L0_cond_all.items() if k in ('W_q', 'b_q', 'W_kv', 'b_kv', 'no_op_k', 'no_op_v', 'W_proj', 'b_proj')}
    del _L0_cond_all

    def _L1_cond_setup():
        import jax, jax.numpy as jnp
        import numpy as np
        B, T, D_IN, V_IN, E = (64, 128, 256, 256, 256)
        key = jax.random.key(seed)
        ks = jax.random.split(key, 16)
        s = 0.01
        return {'video': jax.random.normal(ks[0], (B, V_IN), jnp.float32), 'seq': jax.random.normal(ks[1], (B, T, D_IN), jnp.float32), 'W_z': jax.random.normal(ks[2], (D_IN, E), jnp.float32) * s, 'U_z': jax.random.normal(ks[3], (E, E), jnp.float32) * s, 'C_z': jax.random.normal(ks[4], (V_IN, E), jnp.float32) * s, 'b_z': jnp.zeros((E,), jnp.float32), 'W_r': jax.random.normal(ks[5], (D_IN, E), jnp.float32) * s, 'U_r': jax.random.normal(ks[6], (E, E), jnp.float32) * s, 'C_r': jax.random.normal(ks[7], (V_IN, E), jnp.float32) * s, 'b_r': jnp.zeros((E,), jnp.float32), 'W': jax.random.normal(ks[8], (D_IN, E), jnp.float32) * s, 'U': jax.random.normal(ks[9], (E, E), jnp.float32) * s, 'C': jax.random.normal(ks[10], (V_IN, E), jnp.float32) * s, 'b': jnp.zeros((E,), jnp.float32)}
    _L1_cond_all = _L1_cond_setup()
    _L1_cond_in = {k: v for k, v in _L1_cond_all.items() if k in ('W_z', 'U_z', 'C_z', 'b_z', 'W_r', 'U_r', 'C_r', 'b_r', 'W', 'U', 'C', 'b')}
    del _L1_cond_all
    return {'x': x, 'cond_1024': cond_1024, 'L0_cond_W_q': _L0_cond_in['W_q'], 'L0_cond_b_q': _L0_cond_in['b_q'], 'L0_cond_W_kv': _L0_cond_in['W_kv'], 'L0_cond_b_kv': _L0_cond_in['b_kv'], 'L0_cond_no_op_k': _L0_cond_in['no_op_k'], 'L0_cond_no_op_v': _L0_cond_in['no_op_v'], 'L0_cond_W_proj': _L0_cond_in['W_proj'], 'L0_cond_b_proj': _L0_cond_in['b_proj'], 'L1_cond_W_z': _L1_cond_in['W_z'], 'L1_cond_U_z': _L1_cond_in['U_z'], 'L1_cond_C_z': _L1_cond_in['C_z'], 'L1_cond_b_z': _L1_cond_in['b_z'], 'L1_cond_W_r': _L1_cond_in['W_r'], 'L1_cond_U_r': _L1_cond_in['U_r'], 'L1_cond_C_r': _L1_cond_in['C_r'], 'L1_cond_b_r': _L1_cond_in['b_r'], 'L1_cond_W': _L1_cond_in['W'], 'L1_cond_U': _L1_cond_in['U'], 'L1_cond_C': _L1_cond_in['C'], 'L1_cond_b': _L1_cond_in['b']}

def reference(x, cond_1024, L0_cond_W_q, L0_cond_b_q, L0_cond_W_kv, L0_cond_b_kv, L0_cond_no_op_k, L0_cond_no_op_v, L0_cond_W_proj, L0_cond_b_proj, L1_cond_W_z, L1_cond_U_z, L1_cond_C_z, L1_cond_b_z, L1_cond_W_r, L1_cond_U_r, L1_cond_C_r, L1_cond_b_r, L1_cond_W, L1_cond_U, L1_cond_C, L1_cond_b):
    import jax
    import jax.numpy as jnp

    def _L0_cond_ref(hidden_states, activation, W_q, b_q, W_kv, b_kv, no_op_k, no_op_v, W_proj, b_proj):
        import jax, jax.numpy as jnp
        import numpy as np
        B, S, D = (8, 1024, 256)
        H = 16
        HD = D // H
        ACT_DIM = 256
        b = hidden_states.shape[0]
        q = hidden_states @ W_q + b_q
        q = q.reshape(b, -1, H, HD).transpose(0, 2, 1, 3)
        kv = activation @ W_kv + b_kv
        k1, v1 = (kv[:, :D], kv[:, D:])
        k1 = k1.reshape(b, 1, H, HD).transpose(0, 2, 1, 3)
        v1 = v1.reshape(b, 1, H, HD).transpose(0, 2, 1, 3)
        k = jnp.concatenate([jnp.broadcast_to(no_op_k, (b, H, 1, HD)), k1], axis=2)
        v = jnp.concatenate([jnp.broadcast_to(no_op_v, (b, H, 1, HD)), v1], axis=2)
        scores = jnp.einsum('bhsd,bhkd->bhsk', q, k)
        w = jax.nn.softmax(scores, axis=-1)
        attn = jnp.einsum('bhsk,bhkd->bhsd', w, v)
        attn = attn.transpose(0, 2, 1, 3).reshape(b, -1, D)
        out = attn @ W_proj + b_proj
        return out

    def _L1_cond_ref(video, seq, W_z, U_z, C_z, b_z, W_r, U_r, C_r, b_r, W, U, C, b):
        import jax, jax.numpy as jnp
        import numpy as np
        B, T, D_IN, V_IN, E = (64, 128, 256, 256, 256)
        vz = video @ C_z + b_z
        vr = video @ C_r + b_r
        vh = video @ C + b
        xz = jnp.einsum('btd,de->bte', seq, W_z)
        xr = jnp.einsum('btd,de->bte', seq, W_r)
        xh = jnp.einsum('btd,de->bte', seq, W)

        def step(h, xs):
            xzt, xrt, xht = xs
            z = jax.nn.sigmoid(xzt + h @ U_z + vz)
            r = jax.nn.sigmoid(xrt + h @ U_r + vr)
            hh = jnp.tanh(xht + r * h @ U + vh)
            h_new = (1.0 - z) * h + z * hh
            return (h_new, h_new)
        h0 = jnp.zeros((seq.shape[0], U.shape[0]), seq.dtype)
        xs = (jnp.swapaxes(xz, 0, 1), jnp.swapaxes(xr, 0, 1), jnp.swapaxes(xh, 0, 1))
        _, out_t = jax.lax.scan(step, h0, xs)
        return jnp.swapaxes(out_t, 0, 1)
    x = x + _L0_cond_ref(x, cond_1024, L0_cond_W_q, L0_cond_b_q, L0_cond_W_kv, L0_cond_b_kv, L0_cond_no_op_k, L0_cond_no_op_v, L0_cond_W_proj, L0_cond_b_proj)
    x = x + _L1_cond_ref(cond_1024, x, L1_cond_W_z, L1_cond_U_z, L1_cond_C_z, L1_cond_b_z, L1_cond_W_r, L1_cond_U_r, L1_cond_C_r, L1_cond_b_r, L1_cond_W, L1_cond_U, L1_cond_C, L1_cond_b)
    return x

_drawn_inputs = setup_inputs


def setup_inputs(seed=0):
    import zlib

    import numpy as np

    out = dict(_drawn_inputs(seed))
    spreads = {'L0_cond_b_q': (0.0, 0.8),
     'L0_cond_b_kv': (0.0, 0.464),
     'L0_cond_b_proj': (0.0, 0.1),
     'L1_cond_b_z': (0.0, 2.0),
     'L1_cond_b_r': (0.0, 2.0),
     'L1_cond_b': (0.0, 0.1)}
    factors = {'L0_cond_W_q': 5.168,
     'L0_cond_no_op_k': 8.0,
     'L0_cond_no_op_v': 8.0,
     'L1_cond_W_z': 7.153,
     'L1_cond_U_z': 44.773,
     'L1_cond_C_z': 8.0,
     'L1_cond_W_r': 24.194,
     'L1_cond_U_r': 64.0,
     'L1_cond_C_r': 8.0,
     'L1_cond_U': 4.192}
    for name, (base, spread) in spreads.items():
        noise = np.random.default_rng([zlib.crc32(name.encode()), seed]).standard_normal(out[name].shape)
        drawn = base * np.exp(spread * noise) if base else spread * noise
        out[name] = jnp.asarray(drawn.astype(out[name].dtype))
    for name, factor in factors.items():
        out[name] = (out[name] * factor).astype(out[name].dtype)
    return out
```

```python
from contextlib import ExitStack

import concourse.bass as bass
from concourse import mybir

F32 = mybir.dt.float32
BF16 = mybir.dt.bfloat16
ALU = mybir.AluOpType
ACT = mybir.ActivationFunctionType

P = 128
HEADS = 16
HALF = 8
GB = 8
TS = 16
UNROLL = 4
BQ, NK, NV, BKV, BP, BZ, BR, BC = 0, 2, 4, 6, 10, 12, 14, 16
BIAS_ROWS = 18
Z, R, C = 0, 1, 2


def build(nc, x, cond, consts, W_q, b_q, W_kv, b_kv, no_op_k, no_op_v, W_proj, b_proj,
          W_z, U_z, C_z, b_z, W_r, U_r, C_r, b_r, W, U, C_, b, out):
    B, T, D = x.shape
    KC = D // P
    G = B // GB
    SLICES = T // TS
    PAIRS = TS // 2
    HD = D // HEADS
    assert B == 64 and KC == 2 and HD * HALF == P and GB * HEADS == P and G == 8

    with ExitStack() as ctx:
        def sb(name, shape, dt=F32):
            return ctx.enter_context(nc.sbuf_tensor(name, shape, dt))

        def sem(name):
            return ctx.enter_context(nc.semaphore(name))

        ps = ctx.enter_context(nc.psum_tensor("ps", [P, 8, 512], F32))

        cst = sb("cst", [P, P + HALF + GB])
        ident = cst[:, 0:P]
        head_mask = cst[:, P:P + HALF]
        batch_mask = cst[:, P + HALF:]
        bias_rows = sb("bias_rows", [BIAS_ROWS, P])
        cond_sb = sb("cond_sb", [B, D])
        wq = sb("wq", [P, KC, D])
        wkv = sb("wkv", [P, KC, 2 * D])
        wp = sb("wp", [P, KC, D])
        w_in = [sb(f"w_in{g}", [P, KC, D]) for g in range(3)]
        w_rec = [sb(f"w_rec{g}", [P, KC, D]) for g in range(3)]
        w_cond = [sb(f"w_cond{g}", [P, KC, D]) for g in range(3)]
        xn = sb("xn", [P, 2, PAIRS, D])

        bias = sb("bias", [P, BIAS_ROWS])
        condT = sb("condT", [P, KC, B])
        wqT = sb("wqT", [P, 2, D])
        kv_off = sb("kv_off", [P, 4])
        dkv = sb("dkv", [P, 4, B])
        blk = sb("blk", [P, 4, B, HALF])
        dq = sb("dq", [P, KC, G, 2, GB * HALF])
        s_off = sb("s_off", [P, G])
        nproj = sb("nproj", [P, G, D])
        x_off = sb("x_off", [P, KC])
        vcond = sb("vcond", [P, 3, KC, B])
        zeros = sb("zeros", [P, 512], BF16)

        xT = sb("xT", [P, KC, T, B])
        w1 = sb("w1", [P, G, TS * GB])
        w1m = sb("w1m", [P, G, TS * GB])
        h = sb("h", [P, 2, KC, B])
        r_g = sb("r_g", [P, KC, B])
        z_g = sb("z_g", [P, KC, B])
        c_g = sb("c_g", [P, KC, B])
        rh = sb("rh", [P, KC, B])
        keep = sb("keep", [P, KC, B])
        zc = sb("zc", [P, KC, B])
        y = sb("y", [P, 2, KC, 2, B])
        o_sb = sb("o_sb", [P, T // 2, D])

        small_in = sem("small_in")
        attn_in = sem("attn_in")
        x_in = [sem(f"x_in{s}") for s in range(SLICES)]
        gru_in = sem("gru_in")
        out_done = sem("out_done")
        pe_prep = sem("pe_prep")
        act_prep = sem("act_prep")
        dve_prep = sem("dve_prep")
        turn_ready = sem("turn_ready")
        xT_act = sem("xT_act")
        xT_dve = sem("xT_dve")
        score_ready = sem("score_ready")
        w1_ready = sem("w1_ready")
        w1m_ready = sem("w1m_ready")
        attn_ready = sem("attn_ready")
        x1_ready = sem("x1_ready")
        clean = sem("clean")
        v_ready = sem("v_ready")
        seeded = [sem("seeded_z"), sem("seeded_r"), sem("seeded_c")]
        h_ready = sem("h_ready")
        r_pre = sem("r_pre")
        z_pre = sem("z_pre")
        c_pre = sem("c_pre")
        r_ready = sem("r_ready")
        z_ready = sem("z_ready")
        c_ready = sem("c_ready")
        rh_ready = sem("rh_ready")
        keep_ready = sem("keep_ready")
        zc_ready = sem("zc_ready")
        y_ready = sem("y_ready")
        yT_ready = sem("yT_ready")
        o_ready = sem("o_ready")

        GATE_BANK = {R: 0, Z: 2, C: 4}
        YT_BANK = 6

        def gate(g, m, u):
            return ps[:, GATE_BANK[g] + m, u * B:(u + 1) * B]

        def gate_both(g, u):
            return ps[:, GATE_BANK[g]:GATE_BANK[g] + KC, u * B:(u + 1) * B]

        block = ctx.enter_context(nc.Block())

        @block.sync
        def _(sp):
            sp.dma_start(cst[:], consts).then_inc(small_in, 16)
            sp.dma_start(cond_sb[:], cond).then_inc(small_in, 16)
            for src, at, n in ((b_q, BQ, 2), (no_op_k, NK, 2), (no_op_v, NV, 2), (b_kv, BKV, 4),
                               (b_proj, BP, 2), (b_z, BZ, 2), (b_r, BR, 2), (b, BC, 2)):
                sp.dma_start(bias_rows[at:at + n, :], src).then_inc(small_in, 16)
            for s in range(SLICES):
                if s >= 2:
                    sp.wait_ge(turn_ready, 4 * (s - 1))
                for q in range(2):
                    src = x[:, s * TS:(s + 1) * TS, :].rearrange("b (i q) d -> q b i d", q=2)[q]
                    sp.dma_start(xn[q * B:(q + 1) * B, s % 2], src).then_inc(x_in[s], 16)
            for src, dst in ((C_r, w_cond[R]), (C_z, w_cond[Z]), (C_, w_cond[C])):
                sp.dma_start(dst[:], src.rearrange("(k p) n -> p k n", p=P)).then_inc(gru_in, 16)
            def store(pair):
                sp.wait_ge(o_ready, pair + 1)
                for q in range(2):
                    dst = out.rearrange("b (i q) d -> q b i d", q=2)[q][:, bass.ds(pair, 1), :]
                    sp.dma_start(dst, o_sb[q * B:(q + 1) * B, bass.ds(pair, 1), :]).then_inc(out_done, 16)
            with sp.Fori(0, T // 2) as pair:
                store(pair)
            sp.wait_ge(out_done, 16 * T)

        @block.tensor
        def _(pe):
            mm = nc.tensor.matmul

            pe.wait_ge(small_in, 16 * 10)
            for k in range(KC):
                nc.tensor.transpose(ps[:, 0, k * B:(k + 1) * B], cond_sb[:, k * P:(k + 1) * P], ident[0:B, 0:B])
            nc.tensor.transpose(ps[:, 0, 256:256 + BIAS_ROWS], bias_rows[:],
                                ident[0:BIAS_ROWS, 0:BIAS_ROWS]).then_inc(pe_prep, 1)
            pe.wait_ge(attn_in, 16 * 3)
            for j in range(2):
                for k in range(KC):
                    i = nc.tensor.transpose(ps[:, 1, j * D + k * P:j * D + (k + 1) * P],
                                            wq[:, k, j * P:(j + 1) * P], ident)
            i.then_inc(pe_prep, 1)
            pe.wait_ge(dve_prep, 1)
            for o in range(4):
                for k in range(KC):
                    i = mm(ps[:, 2, o * B:(o + 1) * B], wkv[:, k, o * P:(o + 1) * P], condT[:, k, :],
                           start=(k == 0), stop=(k == KC - 1))
            i.then_inc(pe_prep, 1)
            pe.wait_ge(dve_prep, 2)
            for m in range(KC):
                for j in range(2):
                    mm(ps[:, 3, m:m + 1], wp[:, j, m * P:(m + 1) * P], bias[:, NV + j:NV + j + 1],
                       start=(j == 0), stop=(j == 1))
            pe.wait_ge(dve_prep, 5)
            for g in range(G):
                for j in range(2):
                    i = mm(ps[j * 64:(j + 1) * 64, 3, 8 + g:9 + g], blk[:, j, g * GB:(g + 1) * GB, :],
                           bias[:, BQ + j:BQ + j + 1], start=True, stop=True)
            i.then_inc(pe_prep, 1)
            pe.wait_ge(act_prep, 1)
            for k in range(KC):
                for j in range(2):
                    mm(ps[:, 4 + 2 * k + j, :], wqT[:, j, k * P:(k + 1) * P], blk[:, j],
                       start=True, stop=True).then_inc(pe_prep, 1)
            pe.wait_ge(dve_prep, 6)
            for g in range(G):
                if g == 2:
                    pe.wait_ge(act_prep, 1)
                if g == 4:
                    pe.wait_ge(dve_prep, 7)
                for j in range(2):
                    i = mm(ps[j * 64:(j + 1) * 64, g // 2, (g % 2) * D:(g % 2 + 1) * D],
                           blk[:, 2 + j, g * GB:(g + 1) * GB, :], wp[:, j, :], start=True, stop=True)
                if g % 2:
                    i.then_inc(pe_prep, 1)

            def attention(s, slot):
                for q in range(4):
                    (pe.wait_ge(xT_act, 2 * s + q // 2) if q % 2 == 0 else pe.wait_ge(xT_dve, 2 * s + q // 2))
                    for k in range(KC):
                        for p in range(2):
                            i = nc.tensor.transpose(
                                ps[:, q % 2, k * 256 + p * P:k * 256 + (p + 1) * P],
                                xn[:, slot, 2 * q + p, k * P:(k + 1) * P], ident)
                    i.then_inc(turn_ready, 1)
                pe.wait_ge(xT_act, 2 * s + 2)
                pe.wait_ge(xT_dve, 2 * s + 2)
                for g in range(G):
                    if g == 0:
                        pe.wait_ge(w1_ready, G * s)
                    for k in range(KC):
                        i = mm(ps[:, 2 + g // 4, (g % 4) * P:(g % 4 + 1) * P], dq[:, k, g],
                               xT[:, k, bass.ds(s * TS, TS), g * GB:(g + 1) * GB],
                               start=(k == 0), stop=(k == KC - 1))
                    if g % 4 == 3:
                        i.then_inc(score_ready, 1)
                for gh in range(2):
                    pe.wait_ge(w1m_ready, 2 * s + gh + 1)
                    for m in range(KC):
                        if gh == 0 and m == 0:
                            pe.wait_ge(x1_ready, 4 * s)
                        bank = ps[:, 4 + gh * 2 + m].rearrange("p (t c) -> p t c", c=4 * GB)
                        for gl in range(4):
                            i = mm(bank[:, :, gl * GB:(gl + 1) * GB],
                                   nproj[:, gh * 4 + gl, m * P:(m + 1) * P], w1m[:, gh * 4 + gl],
                                   start=True, stop=True)
                        i.then_inc(attn_ready, 1)

            pe.wait_ge(act_prep, 4)
            pe.wait_ge(dve_prep, 10)
            for s in range(SLICES):
                pe.wait_ge(x_in[s], 32)
                attention(s, s % 2)

            pe.wait_ge(gru_in, 16 * 9)
            pe.wait_ge(x1_ready, 4 * SLICES)
            for g in range(3):
                for m in range(KC):
                    for k in range(KC):
                        i = mm(ps[:, 7, (g * KC + m) * B:(g * KC + m + 1) * B],
                               w_cond[g][:, k, m * P:(m + 1) * P], condT[:, k, :],
                               start=(k == 0), stop=(k == KC - 1))
            i.then_inc(pe_prep, 1)
            for bank in range(6):
                i = mm(ps[:, bank, :], zeros[:, 0:P], zeros[:], start=True, stop=True)
            i.then_inc(clean, 1)

            def add(dst, lhsT, rhs):
                return mm(dst, lhsT, rhs, start=False, stop=False, skip_group_check=True)

            def project(g, t, u):
                for m in range(KC):
                    for k in range(KC):
                        add(gate(g, m, u), w_in[g][:, k, m * P:(m + 1) * P], xT[:, k, bass.ds(t, 1), :])

            def turn_pair(pair, slot):
                pe.wait_ge(y_ready, 2 * pair + 2)
                pe.wait_ge(o_ready, pair)
                for k in range(KC):
                    i = nc.tensor.transpose(ps[:, YT_BANK, k * P:(k + 1) * P], y[:, slot, k], ident)
                i.then_inc(yT_ready, 1)

            def step(t, u, pair_slot, pair, left):
                nxt = (u + 1) % UNROLL
                hs = (u + 1) % 2
                for k in range(KC):
                    pe.wait_ge(h_ready, 2 * t + k + 1)
                    for m in range(KC):
                        i = add(gate(R, m, u), w_rec[R][:, k, m * P:(m + 1) * P], h[:, hs, k])
                        if k == KC - 1:
                            i.then_inc(r_pre, 1)
                for k in range(KC):
                    for m in range(KC):
                        i = add(gate(Z, m, u), w_rec[Z][:, k, m * P:(m + 1) * P], h[:, hs, k])
                i.then_inc(z_pre, 1)
                if left > 0:
                    pe.wait_ge(seeded[C], t + 2)
                    project(C, t + 1, nxt)
                for k in range(KC):
                    pe.wait_ge(rh_ready, 2 * t + k + 1)
                    for m in range(KC):
                        i = add(gate(C, m, u), w_rec[C][:, k, m * P:(m + 1) * P], rh[:, k])
                        if k == KC - 1:
                            i.then_inc(c_pre, 1)
                if left > 0:
                    pe.wait_ge(seeded[R], t + 3 if left > 1 else t + 2)
                    project(R, t + 1, nxt)
                    pe.wait_ge(seeded[Z], t + 3 if left > 1 else t + 2)
                    if left == 1:
                        pe.wait_ge(z_ready, t + 1)
                    project(Z, t + 1, nxt)
                if pair is not None:
                    turn_pair(pair, pair_slot)

            pe.wait_ge(seeded[C], 2)
            project(C, 0, 0)
            pe.wait_ge(seeded[R], 2)
            project(R, 0, 0)
            pe.wait_ge(seeded[Z], 2)
            project(Z, 0, 0)
            step(0, 0, 0, None, T - 1)
            LOOPS = (T - 1) // UNROLL
            with pe.Fori(0, LOOPS) as i4:
                for n in range(UNROLL):
                    even = (n + 1) % 2 == 0
                    step(UNROLL * i4 + n + 1, (n + 1) % UNROLL, (n // 2) % 2,
                         2 * i4 + n // 2 if even else None, 99)
            for t in range(LOOPS * UNROLL + 1, T):
                pair = t // 2 - 1
                step(t, t % UNROLL, pair % 2, pair if t % 2 == 0 else None, T - 1 - t)
            turn_pair(T // 2 - 1, (T // 2 - 1) % 2)

        @block.scalar
        def _(act):
            for src, dst in ((W_kv, wkv), (W_q, wq), (W_proj, wp)):
                act.dma_start(dst[:], src.rearrange("(k p) n -> p k n", p=P)).then_inc(attn_in, 16)
            for src, dst in ((W_r, w_in[R]), (W_z, w_in[Z]), (W, w_in[C]), (U_r, w_rec[R]),
                             (U_z, w_rec[Z]), (U, w_rec[C])):
                act.dma_start(dst[:], src.rearrange("(k p) n -> p k n", p=P)).then_inc(gru_in, 16)
            act.wait_ge(pe_prep, 2)
            nc.scalar.copy(wqT[:].rearrange("p j c -> p (j c)"), ps[:, 1, :]).then_inc(act_prep, 1)
            act.wait_ge(pe_prep, 6)
            nc.scalar.copy(dq[:, 0, :, 0, :], ps[:, 4].rearrange("p (g n) -> p g n", g=G))
            nc.scalar.copy(dq[:, 0, :, 1, :], ps[:, 5].rearrange("p (g n) -> p g n", g=G)).then_inc(act_prep, 1)
            for n in range(2):
                act.wait_ge(pe_prep, 9 + n)
                nc.scalar.copy(nproj[:, 2 * n:2 * n + 2, :].rearrange("p g e -> p (g e)"),
                               ps[:, n, :]).then_inc(act_prep, 1)

            def attention(s):
                for q in (0, 2):
                    act.wait_ge(turn_ready, 4 * s + q + 1)
                    nc.scalar.copy(
                        xT[:, :, bass.ds(s * TS + 4 * q, 4), :].rearrange("p k t b -> p k (t b)"),
                        ps[:, 0].rearrange("p (k n) -> p k n", k=KC)).then_inc(xT_act, 1)
                for g in range(G):
                    act.wait_ge(score_ready, 2 * s + g // 4 + 1)
                    if g % 4 == 0:
                        act.wait_ge(w1m_ready, 2 * s)
                    nc.scalar.activation(w1[:, g], ps[:, 2 + g // 4, (g % 4) * P:(g % 4 + 1) * P],
                                         ACT.Sigmoid, bias=s_off[:, g:g + 1]).then_inc(w1_ready, 1)

            act.wait_ge(dve_prep, 7)
            with act.Fori(0, SLICES) as s:
                attention(s)

            def seed(g, u, n=1):
                for k in range(n):
                    i = nc.scalar.copy(gate_both(g, u + k), vcond[:, g])
                i.then_inc(seeded[g], n)

            act.wait_ge(v_ready, 1)
            act.wait_ge(clean, 1)
            for g in (C, R, Z):
                seed(g, 0, 2)

            def step(t, u, left):
                ahead = (u + 2) % UNROLL
                for m in range(KC):
                    act.wait_ge(r_pre, 2 * t + m + 1)
                    nc.scalar.activation(r_g[:, m], gate(R, m, u), ACT.Sigmoid).then_inc(r_ready, 1)
                if left > 1:
                    seed(R, ahead)
                act.wait_ge(z_pre, t + 1)
                nc.scalar.activation(z_g[:], gate_both(Z, u), ACT.Sigmoid).then_inc(z_ready, 1)
                if left > 1:
                    seed(Z, ahead)
                for m in range(KC):
                    act.wait_ge(c_pre, 2 * t + m + 1)
                    nc.scalar.activation(c_g[:, m], gate(C, m, u), ACT.Tanh).then_inc(c_ready, 1)
                if left > 1:
                    seed(C, ahead)

            def copy_pair(pair):
                act.wait_ge(yT_ready, pair + 1)
                nc.scalar.copy(o_sb[:, bass.ds(pair, 1), :].rearrange("p i e -> p (i e)"),
                               ps[:, YT_BANK, 0:D]).then_inc(o_ready, 1)

            step(0, 0, T - 1)
            LOOPS = (T - 1) // UNROLL
            with act.Fori(0, LOOPS) as i4:
                for n in range(UNROLL):
                    step(UNROLL * i4 + n + 1, (n + 1) % UNROLL, 99)
                    if n % 2:
                        copy_pair(2 * i4 + n // 2)
            for t in range(LOOPS * UNROLL + 1, T):
                step(t, t % UNROLL, T - 1 - t)
                if t % 2 == 0:
                    copy_pair(t // 2 - 1)
            copy_pair(T // 2 - 1)

        @block.vector
        def _(dve):
            def per_column(v, n):
                return v.rearrange("p (c u) -> p c u", u=1).broadcast_to([P, v.shape[1], n])

            nc.vector.memset(zeros[:], 0.0)
            dve.wait_ge(pe_prep, 1)
            nc.vector.tensor_copy(condT[:].rearrange("p k b -> p (k b)"),
                                  ps[:, 0, 0:KC * B]).then_inc(dve_prep, 1)
            nc.vector.tensor_copy(bias[:], ps[:, 0, 256:256 + BIAS_ROWS]).then_inc(dve_prep, 1)
            dve.wait_ge(dve_prep, 2)
            nc.vector.tensor_tensor(kv_off[:], bias[:, BKV:BKV + 4], bias[:, NK:NK + 4],
                                    ALU.subtract).then_inc(dve_prep, 1)
            dve.wait_ge(dve_prep, 3)
            dve.wait_ge(pe_prep, 3)
            nc.vector.tensor_tensor(dkv[:], ps[:, 2, 0:4 * B].rearrange("p (o b) -> p o b", o=4),
                                    per_column(kv_off[:], B), ALU.add).then_inc(dve_prep, 1)
            dve.wait_ge(dve_prep, 4)
            for first in (0, 2):
                for o in (first, first + 1):
                    i = nc.vector.tensor_tensor(
                        blk[:, o], per_column(dkv[:, o], HALF),
                        head_mask.rearrange("p (u h) -> p u h", u=1).broadcast_to([P, B, HALF]), ALU.mult)
                i.then_inc(dve_prep, 1)
            dve.wait_ge(pe_prep, 4)
            nc.vector.tensor_copy(s_off[:], ps[:, 3, 8:8 + G])
            nc.vector.tensor_tensor(x_off[:], ps[:, 3, 0:KC], bias[:, BP:BP + KC],
                                    ALU.add).then_inc(dve_prep, 1)
            dve.wait_ge(pe_prep, 8)
            for j in range(2):
                i = nc.vector.tensor_copy(dq[:, 1, :, j, :], ps[:, 6 + j].rearrange("p (g n) -> p g n", g=G))
            i.then_inc(dve_prep, 1)
            for n in range(2):
                dve.wait_ge(pe_prep, 11 + n)
                nc.vector.tensor_copy(nproj[:, 4 + 2 * n:6 + 2 * n, :].rearrange("p g e -> p (g e)"),
                                      ps[:, 2 + n, :]).then_inc(dve_prep, 1)
            dve.wait_ge(dve_prep, 10)

            with dve.Fori(0, SLICES) as s:
                for q in (1, 3):
                    dve.wait_ge(turn_ready, 4 * s + q + 1)
                    nc.vector.tensor_copy(
                        xT[:, :, bass.ds(s * TS + 4 * q, 4), :].rearrange("p k t b -> p k (t b)"),
                        ps[:, 1].rearrange("p (k n) -> p k n", k=KC)).then_inc(xT_dve, 1)
                for gh in range(2):
                    dve.wait_ge(w1_ready, G * s + 4 * gh + 4)
                    if gh == 0:
                        dve.wait_ge(attn_ready, 4 * s)
                    nc.vector.tensor_tensor(
                        w1m[:, 4 * gh:4 * gh + 4].rearrange("p g (t b) -> p (g t) b", b=GB),
                        w1[:, 4 * gh:4 * gh + 4].rearrange("p g (t b) -> p (g t) b", b=GB),
                        batch_mask.rearrange("p (u b) -> p u b", u=1).broadcast_to([P, 4 * TS, GB]),
                        ALU.mult).then_inc(w1m_ready, 1)
                for gh in range(2):
                    for m in range(KC):
                        dve.wait_ge(attn_ready, 4 * s + 2 * gh + m + 1)
                        x_cols = xT[:, m, bass.ds(s * TS, TS), 4 * GB * gh:4 * GB * (gh + 1)]
                        nc.vector.scalar_tensor_tensor(
                            out=x_cols, in0=ps[:, 4 + 2 * gh + m].rearrange("p (t c) -> p t c", t=TS),
                            scalar=x_off[:, m:m + 1], in1=x_cols,
                            op0=ALU.add, op1=ALU.add).then_inc(x1_ready, 1)

            dve.wait_ge(pe_prep, 13)
            nc.vector.tensor_tensor(
                vcond[:].rearrange("p g k b -> p (g k) b"),
                ps[:, 7, 0:6 * B].rearrange("p (o b) -> p o b", o=6),
                per_column(bias[:, BZ:BZ + 6], B), ALU.add).then_inc(v_ready, 1)
            nc.vector.memset(h[:, 1], 0.0).then_inc(h_ready, 2)

            def step(t, u):
                now, last = u % 2, (u + 1) % 2
                for k in range(KC):
                    dve.wait_ge(r_ready, 2 * t + k + 1)
                    nc.vector.tensor_tensor(rh[:, k], r_g[:, k], h[:, last, k], ALU.mult).then_inc(rh_ready, 1)
                dve.wait_ge(z_ready, t + 1)
                nc.vector.scalar_tensor_tensor(out=keep[:], in0=z_g[:], scalar=1.0, in1=h[:, last],
                                               op0=ALU.subtract, op1=ALU.mult).then_inc(keep_ready, 1)
                dve.wait_ge(y_ready, t)
                dve.wait_ge(keep_ready, t + 1)
                for k in range(KC):
                    dve.wait_ge(c_ready, 2 * t + k + 1)
                    nc.vector.tensor_tensor(zc[:, k], z_g[:, k], c_g[:, k], ALU.mult).then_inc(zc_ready, 1)
                    dve.wait_ge(zc_ready, 2 * t + k + 1)
                    nc.vector.tensor_tensor(h[:, now, k], zc[:, k], keep[:, k],
                                            ALU.subtract).then_inc(h_ready, 1)

            step(0, 0)
            LOOPS = (T - 1) // UNROLL
            with dve.Fori(0, LOOPS) as i4:
                for n in range(UNROLL):
                    step(UNROLL * i4 + n + 1, (n + 1) % UNROLL)
            for t in range(LOOPS * UNROLL + 1, T):
                step(t, t % UNROLL)

        @block.gpsimd
        def _(pool):
            pool.wait_ge(x1_ready, 4 * SLICES)

            def residual(t, pair, par, slot):
                pool.wait_ge(h_ready, 2 * t + 4)
                pool.wait_ge(yT_ready, pair)
                nc.gpsimd.tensor_tensor(y[:, slot, :, par], xT[:, :, bass.ds(t, 1), :].rearrange("p k t b -> p k (t b)"),
                                        h[:, par], ALU.add).then_inc(y_ready, 1)

            with pool.Fori(0, T // 4) as i4:
                for n in range(4):
                    residual(4 * i4 + n, 2 * i4 + n // 2, n % 2, n // 2)


_INS = ["x", "cond_1024", "L0_cond_W_q", "L0_cond_b_q", "L0_cond_W_kv", "L0_cond_b_kv",
        "L0_cond_no_op_k", "L0_cond_no_op_v", "L0_cond_W_proj", "L0_cond_b_proj",
        "L1_cond_W_z", "L1_cond_U_z", "L1_cond_C_z", "L1_cond_b_z",
        "L1_cond_W_r", "L1_cond_U_r", "L1_cond_C_r", "L1_cond_b_r",
        "L1_cond_W", "L1_cond_U", "L1_cond_C", "L1_cond_b"]
_ROWS = {"b_q", "b_kv", "no_op_k", "no_op_v", "b_proj", "b_z", "b_r", "b"}


def kernel(**inputs):
    import numpy as np
    import concourse.bacc as bacc
    from concourse.bass_utils import run_bass_kernel_spmd

    nc = bacc.Bacc("TRN2", target_bir_lowering=False, num_devices=1)
    arrays, args = {}, []

    def give(name, a):
        a = np.ascontiguousarray(a)
        arrays[name] = a
        return nc.dram_tensor(name, a.shape, mybir.dt.from_np(a.dtype), kind="ExternalInput").ap()

    p = np.arange(P)
    consts = np.concatenate([np.eye(P), p[:, None] // 16 == np.arange(HALF),
                             p[:, None] // HALF % GB == np.arange(GB)], axis=1).astype(np.float32)
    for name in _INS:
        a = np.asarray(inputs[name])
        if name.split("cond_", 1)[-1] in _ROWS:
            a = a.reshape(-1, P)
        args.append(give("in_" + name, a))
        if name == "cond_1024":
            args.append(give("in_consts", consts))
    shape = np.asarray(inputs["x"]).shape
    args.append(nc.dram_tensor("out_0", shape, F32, kind="ExternalOutput").ap())
    build(nc, *args)
    r = run_bass_kernel_spmd(nc, [arrays], core_ids=[0])
    return r.results[0]["out_0"]
```

```python
from contextlib import ExitStack

import concourse.bass as bass
from concourse import mybir

F32 = mybir.dt.float32
F32R = mybir.dt.float32r
BF16 = mybir.dt.bfloat16
ALU = mybir.AluOpType
ACT = mybir.ActivationFunctionType

P = 128
HEADS = 16
HALF = 8
GB = 8
TS = 16
GS = 4
BQ, NK, NV, BKV, BP, BZ, BR, BC = 0, 2, 4, 6, 10, 12, 14, 16
BIAS_ROWS = 18
Z, R, C = 0, 1, 2


def build(nc, x, cond, consts, W_q, b_q, W_kv, b_kv, no_op_k, no_op_v, W_proj, b_proj,
          W_z, U_z, C_z, b_z, W_r, U_r, C_r, b_r, W, U, C_, b, out):
    B, T, D = x.shape
    KC = D // P
    G = B // GB
    SLICES = T // TS
    PAIRS = TS // 2
    HD = D // HEADS
    assert B == 64 and KC == 2 and HD * HALF == P and GB * HEADS == P and G == 8

    with ExitStack() as ctx:
        def sb(name, shape, dt=F32):
            return ctx.enter_context(nc.sbuf_tensor(name, shape, dt))

        def sem(name):
            return ctx.enter_context(nc.semaphore(name))

        ps = ctx.enter_context(nc.psum_tensor("ps", [P, 8, 512], F32))

        cst = sb("cst", [P, P + HALF + GB])
        ident = cst[:, 0:P]
        head_mask = cst[:, P:P + HALF]
        batch_mask = cst[:, P + HALF:]
        bias_rows = sb("bias_rows", [BIAS_ROWS, P])
        cond_sb = sb("cond_sb", [B, D])
        wq = sb("wq", [P, KC, D])
        wkv = sb("wkv", [P, KC, 2 * D])
        wp = sb("wp", [P, KC, D])
        w_in = [sb(f"w_in{g}", [P, KC, D]) for g in range(3)]
        w_rec = [sb(f"w_rec{g}", [P, KC, D]) for g in range(3)]
        w_hi = [sb(f"w_hi{g}", [P, KC, D], F32R) for g in range(3)]
        w_lo = [sb(f"w_lo{g}", [P, KC, D], F32R) for g in range(3)]
        u_part = [[sb(f"u{g}_{n}", [P, KC, D], BF16) for n in range(3)] for g in range(3)]
        w_cond = [sb(f"w_cond{g}", [P, KC, D]) for g in range(3)]
        xn = sb("xn", [P, 2, PAIRS, D])

        bias = sb("bias", [P, BIAS_ROWS])
        condT = sb("condT", [P, KC, B])
        wqT = sb("wqT", [P, 2, D])
        kv_off = sb("kv_off", [P, 4])
        dkv = sb("dkv", [P, 4, B])
        blk = sb("blk", [P, 4, B, HALF])
        dq = sb("dq", [P, KC, G, 2, GB * HALF])
        s_off = sb("s_off", [P, G])
        nproj = sb("nproj", [P, G, D])
        x_off = sb("x_off", [P, KC])
        vcond = sb("vcond", [P, 3, KC, B])
        zeros = sb("zeros", [P, 512], BF16)

        xT = sb("xT", [P, KC, T, B])
        x_hi = sb("x_hi", [P, KC, T, B], F32R)
        x_lo = sb("x_lo", [P, KC, T, B], F32R)
        w1 = sb("w1", [P, G, TS * GB])
        w1m = sb("w1m", [P, G, TS * GB])
        h = sb("h", [P, 2, KC, B])
        r_g = sb("r_g", [P, KC, B])
        z_g = sb("z_g", [P, KC, B])
        c_g = sb("c_g", [P, KC, B])
        rh = sb("rh", [P, KC, B])
        h_rest = sb("h_rest", [P, KC, B])
        h_last = sb("h_last", [P, KC, B], BF16)
        rh_rest = sb("rh_rest", [P, KC, B])
        rh_last = sb("rh_last", [P, KC, B], BF16)
        keep = sb("keep", [P, KC, B])
        zc = sb("zc", [P, KC, B])
        y = sb("y", [P, 2, KC, 2, B])

        small_in = sem("small_in")
        attn_in = sem("attn_in")
        x_in = [sem(f"x_in{s}") for s in range(SLICES)]
        gru_in = sem("gru_in")
        out_done = sem("out_done")
        pe_prep = sem("pe_prep")
        act_prep = sem("act_prep")
        dve_prep = sem("dve_prep")
        turn_ready = sem("turn_ready")
        xT_act = sem("xT_act")
        xT_dve = sem("xT_dve")
        score_ready = sem("score_ready")
        w1_ready = sem("w1_ready")
        w1m_ready = sem("w1m_ready")
        attn_ready = sem("attn_ready")
        x1_ready = sem("x1_ready")
        clean = sem("clean")
        v_ready = sem("v_ready")
        seeded = [sem("seeded_z"), sem("seeded_r"), sem("seeded_c")]
        h_ready = sem("h_ready")
        r_pre = sem("r_pre")
        z_pre = sem("z_pre")
        c_pre = sem("c_pre")
        r_ready = sem("r_ready")
        z_ready = sem("z_ready")
        c_ready = sem("c_ready")
        h_rest_ready = sem("h_rest_ready")
        h_last_ready = sem("h_last_ready")
        rh_ready = sem("rh_ready")
        rh_rest_ready = sem("rh_rest_ready")
        rh_last_ready = sem("rh_last_ready")
        x_hi_ready = sem("x_hi_ready")
        x_lo_ready = sem("x_lo_ready")
        split = sem("split")
        w_split = sem("w_split")
        keep_ready = sem("keep_ready")
        zc_ready = sem("zc_ready")
        y_ready = sem("y_ready")
        yT_ready = sem("yT_ready")
        o_ready = sem("o_ready")

        GATE_BANK = {R: 0, Z: 2, C: 4}
        YT_BANK = 6
        GROUPS = T // GS
        assert GROUPS % 2 == 0 and GROUPS >= 4

        def gate(g, m, par, v, n=1):
            at = (par * GS + v) * B
            return ps[:, GATE_BANK[g] + m, at:at + n * B]

        def gate_both(g, par, v, n=1):
            at = (par * GS + v) * B
            return ps[:, GATE_BANK[g]:GATE_BANK[g] + KC, at:at + n * B]

        def top(ap):
            return ap.bitcast(BF16)[:, 1::2]

        def pair_of(p):
            return xT[:, :, bass.ds(2 * p, 2), :].rearrange("p k t b -> p k (t b)")

        def groups(eng, body):
            body(0, 0, first=True)
            with eng.Fori(0, GROUPS // 2 - 1) as i:
                body(2 * i + 1, 1)
                body(2 * i + 2, 0)
            body(GROUPS - 1, 1, last=True)

        block = ctx.enter_context(nc.Block())

        @block.sync
        def _(sp):
            sp.dma_start(cst[:], consts).then_inc(small_in, 16)
            sp.dma_start(cond_sb[:], cond).then_inc(small_in, 16)
            for src, at, n in ((b_q, BQ, 2), (no_op_k, NK, 2), (no_op_v, NV, 2), (b_kv, BKV, 4),
                               (b_proj, BP, 2), (b_z, BZ, 2), (b_r, BR, 2), (b, BC, 2)):
                sp.dma_start(bias_rows[at:at + n, :], src).then_inc(small_in, 16)
            for s in range(SLICES):
                if s >= 2:
                    sp.wait_ge(turn_ready, 4 * (s - 1))
                for q in range(2):
                    src = x[:, s * TS:(s + 1) * TS, :].rearrange("b (i q) d -> q b i d", q=2)[q]
                    sp.dma_start(xn[q * B:(q + 1) * B, s % 2], src).then_inc(x_in[s], 16)
            for src, dst in ((C_r, w_cond[R]), (C_z, w_cond[Z]), (C_, w_cond[C])):
                sp.dma_start(dst[:], src.rearrange("(k p) n -> p k n", p=P)).then_inc(gru_in, 16)
            with sp.Fori(0, T // 2) as pair:
                sp.wait_ge(o_ready, pair + 1)
                for q in range(2):
                    dst = out.rearrange("b (i q) (k e) -> q b i k e", q=2, k=KC)[q][:, bass.ds(pair, 1)]
                    src = pair_of(pair)[q * B:(q + 1) * B]
                    sp.dma_start(dst.rearrange("b i k e -> b (i k) e"), src).then_inc(out_done, 16)
            sp.wait_ge(out_done, 16 * T)

        @block.tensor
        def _(pe):
            mm = nc.tensor.matmul

            pe.wait_ge(small_in, 16 * 10)
            for k in range(KC):
                nc.tensor.transpose(ps[:, 0, k * B:(k + 1) * B], cond_sb[:, k * P:(k + 1) * P], ident[0:B, 0:B])
            nc.tensor.transpose(ps[:, 0, 256:256 + BIAS_ROWS], bias_rows[:],
                                ident[0:BIAS_ROWS, 0:BIAS_ROWS]).then_inc(pe_prep, 1)
            pe.wait_ge(attn_in, 16 * 3)
            for j in range(2):
                for k in range(KC):
                    i = nc.tensor.transpose(ps[:, 1, j * D + k * P:j * D + (k + 1) * P],
                                            wq[:, k, j * P:(j + 1) * P], ident)
            i.then_inc(pe_prep, 1)
            pe.wait_ge(dve_prep, 1)
            for o in range(4):
                for k in range(KC):
                    i = mm(ps[:, 2, o * B:(o + 1) * B], wkv[:, k, o * P:(o + 1) * P], condT[:, k, :],
                           start=(k == 0), stop=(k == KC - 1))
            i.then_inc(pe_prep, 1)
            pe.wait_ge(dve_prep, 2)
            for m in range(KC):
                for j in range(2):
                    mm(ps[:, 3, m:m + 1], wp[:, j, m * P:(m + 1) * P], bias[:, NV + j:NV + j + 1],
                       start=(j == 0), stop=(j == 1))
            pe.wait_ge(dve_prep, 5)
            for g in range(G):
                for j in range(2):
                    i = mm(ps[j * 64:(j + 1) * 64, 3, 8 + g:9 + g], blk[:, j, g * GB:(g + 1) * GB, :],
                           bias[:, BQ + j:BQ + j + 1], start=True, stop=True)
            i.then_inc(pe_prep, 1)
            pe.wait_ge(act_prep, 1)
            for k in range(KC):
                for j in range(2):
                    mm(ps[:, 4 + 2 * k + j, :], wqT[:, j, k * P:(k + 1) * P], blk[:, j],
                       start=True, stop=True).then_inc(pe_prep, 1)
            pe.wait_ge(dve_prep, 6)
            for g in range(G):
                if g == 2:
                    pe.wait_ge(act_prep, 1)
                if g == 4:
                    pe.wait_ge(dve_prep, 7)
                for j in range(2):
                    i = mm(ps[j * 64:(j + 1) * 64, g // 2, (g % 2) * D:(g % 2 + 1) * D],
                           blk[:, 2 + j, g * GB:(g + 1) * GB, :], wp[:, j, :], start=True, stop=True)
                if g % 2:
                    i.then_inc(pe_prep, 1)

            def turn(s):
                pe.wait_ge(x_in[s], 32)
                for q in range(4):
                    if q == 0 and s == 0:
                        pe.wait_ge(act_prep, 4)
                        pe.wait_ge(dve_prep, 10)
                    elif q % 2 == 0:
                        pe.wait_ge(xT_act, 2 * s + q // 2)
                    elif 2 * s + q // 2:
                        pe.wait_ge(xT_dve, 2 * s + q // 2)
                    for k in range(KC):
                        for p in range(2):
                            i = nc.tensor.transpose(
                                ps[:, q % 2, k * 256 + p * P:k * 256 + (p + 1) * P],
                                xn[:, s % 2, 2 * q + p, k * P:(k + 1) * P], ident)
                    i.then_inc(turn_ready, 1)

            turn(0)
            for s in range(SLICES):
                pe.wait_ge(xT_act, 2 * s + 2)
                pe.wait_ge(xT_dve, 2 * s + 2)
                if s:
                    pe.wait_ge(w1_ready, G * s)
                for g in range(G):
                    for k in range(KC):
                        i = mm(ps[:, 2 + g // 4, (g % 4) * P:(g % 4 + 1) * P], dq[:, k, g],
                               xT[:, k, s * TS:(s + 1) * TS, g * GB:(g + 1) * GB],
                               start=(k == 0), stop=(k == KC - 1))
                    if g % 4 == 3:
                        i.then_inc(score_ready, 1)
                if s < SLICES - 1:
                    turn(s + 1)
                for gh in range(2):
                    pe.wait_ge(w1m_ready, 2 * s + gh + 1)
                    for m in range(KC):
                        if gh == 0 and m == 0 and s:
                            pe.wait_ge(x1_ready, 4 * s)
                        bank = ps[:, 4 + gh * 2 + m].rearrange("p (t c) -> p t c", c=4 * GB)
                        for gl in range(4):
                            i = mm(bank[:, :, gl * GB:(gl + 1) * GB],
                                   nproj[:, gh * 4 + gl, m * P:(m + 1) * P], w1m[:, gh * 4 + gl],
                                   start=True, stop=True)
                        i.then_inc(attn_ready, 1)

            pe.wait_ge(gru_in, 16 * 9)
            pe.wait_ge(x1_ready, 4 * SLICES)
            for g in range(3):
                for m in range(KC):
                    for k in range(KC):
                        i = mm(ps[:, 7, (g * KC + m) * B:(g * KC + m + 1) * B],
                               w_cond[g][:, k, m * P:(m + 1) * P], condT[:, k, :],
                               start=(k == 0), stop=(k == KC - 1))
            i.then_inc(pe_prep, 1)
            for bank in range(6):
                i = mm(ps[:, bank, :], zeros[:, 0:P], zeros[:], start=True, stop=True)
            i.then_inc(clean, 1)

            def add(dst, lhsT, rhs):
                return mm(dst, lhsT, rhs, start=False, stop=False, skip_group_check=True)

            def project(g, m, k, grp, par):
                for w, xp in ((w_hi, x_hi), (w_lo, x_hi), (w_hi, x_lo)):
                    add(gate(g, m, par, 0, GS), w[g][:, k, m * P:(m + 1) * P],
                        xp[:, k, bass.ds(grp * GS, GS), :].rearrange("p t b -> p (t b)"))

            def recur(g, par, v, whole, rest, last, waits, done):
                for n, (part, used) in enumerate(((whole, 3), (rest, 2), (last, 1))):
                    for k in range(KC):
                        if waits:
                            pe.wait_ge(waits[n], waits[3] + k + 1)
                        moving = part[:, k] if n == 2 else top(part[:, k])
                        for w in range(used):
                            for m in range(KC):
                                i = add(gate(g, m, par, v), u_part[g][w][:, k, m * P:(m + 1) * P], moving)
                                if n == 2 and k == KC - 1 and done and (done[1] or m == KC - 1):
                                    i.then_inc(done[0], 1)

            PLAN = [[(R, 0, 0), (R, 0, 1), (R, 1, 0)],
                    [(R, 1, 1), (Z, 0, 0), (Z, 0, 1)],
                    [(Z, 1, 0), (C, 0, 0), (C, 0, 1)],
                    [(Z, 1, 1), (C, 1, 0), (C, 1, 1)]]

            def group(grp, par, first=False, last=False):
                for v in range(GS):
                    t = GS * grp + v
                    h_prev = h[:, (v + 1) % 2]
                    recur(R, par, v, h_prev, h_rest, h_last,
                          (h_ready, h_rest_ready, h_last_ready, 2 * t), (r_pre, True))
                    recur(Z, par, v, h_prev, h_rest, h_last, None, (z_pre, False))
                    if not (first and v < 2):
                        slot = (v // 2 + 1) % 2
                        pair = 2 * grp + v // 2 - 1
                        if v % 2 == 0:
                            pe.wait_ge(y_ready, 2 * pair + 2)
                            if not first:
                                pe.wait_ge(o_ready, pair)
                        i = nc.tensor.transpose(ps[:, YT_BANK, (v % 2) * P:(v % 2 + 1) * P],
                                                y[:, slot, v % 2].rearrange("p t b -> p (t b)"), ident)
                        if v % 2:
                            i.then_inc(yT_ready, 1)
                    recur(C, par, v, rh, rh_rest, rh_last,
                          (rh_ready, rh_rest_ready, rh_last_ready, 2 * t), (c_pre, True))
                    if not last:
                        for g, m, k in PLAN[v]:
                            if (g, m, k) in ((R, 0, 0), (Z, 0, 0), (C, 0, 0)):
                                pe.wait_ge(seeded[g], grp + 2)
                            if (g, m, k) == (Z, 0, 0):
                                pe.wait_ge(z_ready, t + 1)
                            elif (g, m, k) == (Z, 1, 0) or (g, m, k) == (Z, 1, 1):
                                pe.wait_ge(z_ready, t + 1)
                            elif g == C and (k == 0 or v == 3):
                                pe.wait_ge(c_ready, 2 * t + m + 1)
                            project(g, m, k, grp + 1, 1 - par)

            pe.wait_ge(x_lo_ready, 4 * SLICES)
            pe.wait_ge(w_split, 3)
            for g in (R, Z, C):
                pe.wait_ge(seeded[g], 1)
                for m in range(KC):
                    for k in range(KC):
                        project(g, m, k, 0, 0)
            pe.wait_ge(w_split, 6)
            groups(pe, group)
            pe.wait_ge(y_ready, T)
            pe.wait_ge(o_ready, T // 2 - 1)
            for k in range(KC):
                i = nc.tensor.transpose(ps[:, YT_BANK, k * P:(k + 1) * P],
                                        y[:, 1, k].rearrange("p t b -> p (t b)"), ident)
            i.then_inc(yT_ready, 1)

        @block.scalar
        def _(act):
            for src, dst in ((W_kv, wkv), (W_q, wq), (W_proj, wp)):
                act.dma_start(dst[:], src.rearrange("(k p) n -> p k n", p=P)).then_inc(attn_in, 16)
            for src, dst in ((W_r, w_in[R]), (W_z, w_in[Z]), (W, w_in[C]), (U_r, w_rec[R]),
                             (U_z, w_rec[Z]), (U, w_rec[C])):
                act.dma_start(dst[:], src.rearrange("(k p) n -> p k n", p=P)).then_inc(gru_in, 16)
            act.wait_ge(pe_prep, 2)
            nc.scalar.copy(wqT[:].rearrange("p j c -> p (j c)"), ps[:, 1, :]).then_inc(act_prep, 1)
            act.wait_ge(pe_prep, 6)
            nc.scalar.copy(dq[:, 0, :, 0, :], ps[:, 4].rearrange("p (g n) -> p g n", g=G))
            nc.scalar.copy(dq[:, 0, :, 1, :], ps[:, 5].rearrange("p (g n) -> p g n", g=G)).then_inc(act_prep, 1)
            for n in range(2):
                act.wait_ge(pe_prep, 9 + n)
                nc.scalar.copy(nproj[:, 2 * n:2 * n + 2, :].rearrange("p g e -> p (g e)"),
                               ps[:, n, :]).then_inc(act_prep, 1)

            def turned(s, which=(0, 2)):
                for q in which:
                    act.wait_ge(turn_ready, 4 * s + q + 1)
                    nc.scalar.copy(
                        xT[:, :, bass.ds(s * TS + 4 * q, 4), :].rearrange("p k t b -> p k (t b)"),
                        ps[:, 0].rearrange("p (k n) -> p k n", k=KC)).then_inc(xT_act, 1)

            def softmax(s, gh):
                for g in range(4 * gh, 4 * gh + 4):
                    if g % 4 == 0:
                        act.wait_ge(score_ready, 2 * s + g // 4 + 1)
                    nc.scalar.activation(w1[:, g], ps[:, 2 + g // 4, (g % 4) * P:(g % 4 + 1) * P],
                                         ACT.Sigmoid, bias=s_off[:, g:g + 1]).then_inc(w1_ready, 1)

            def round_x1(s):
                for gh in range(2):
                    for m in range(KC):
                        act.wait_ge(x1_ready, 4 * s + 2 * gh + m + 1)
                        cols = slice(4 * GB * gh, 4 * GB * (gh + 1))
                        nc.scalar.copy(x_hi[:, m, bass.ds(s * TS, TS), cols],
                                       xT[:, m, bass.ds(s * TS, TS), cols]).then_inc(x_hi_ready, 1)

            act.wait_ge(dve_prep, 7)
            turned(0)
            with act.Fori(0, SLICES - 1) as s:
                softmax(s, 0)
                turned(s + 1, (0,))
                softmax(s, 1)
                turned(s + 1, (2,))
                round_x1(s)
            softmax(SLICES - 1, 0)
            softmax(SLICES - 1, 1)
            round_x1(SLICES - 1)

            def seed(g, par):
                for m in range(KC):
                    i = nc.scalar.copy(
                        gate(g, m, par, 0, GS).rearrange("p (t b) -> p t b", t=GS),
                        vcond[:, g, m].rearrange("p (u b) -> p u b", u=1).broadcast_to([P, GS, B]))
                i.then_inc(seeded[g], 1)

            act.wait_ge(v_ready, 1)
            act.wait_ge(clean, 1)
            for g in (R, Z, C):
                seed(g, 0)

            def copy_pair(pair):
                act.wait_ge(yT_ready, pair + 1)
                nc.scalar.copy(pair_of(pair), ps[:, YT_BANK, 0:D].rearrange("p (k e) -> p k e", k=KC)
                               ).then_inc(o_ready, 1)

            def group(grp, par, first=False, last=False):
                for v in range(GS):
                    t = GS * grp + v
                    for m in range(KC):
                        act.wait_ge(r_pre, 2 * t + m + 1)
                        nc.scalar.activation(r_g[:, m], gate(R, m, par, v), ACT.Sigmoid).then_inc(r_ready, 1)
                    if v == 0 and not last:
                        seed(R, 1 - par)
                    act.wait_ge(z_pre, t + 1)
                    nc.scalar.activation(z_g[:], gate_both(Z, par, v), ACT.Sigmoid).then_inc(z_ready, 1)
                    if v == 0 and not last:
                        seed(Z, 1 - par)
                    for m in range(KC):
                        act.wait_ge(c_pre, 2 * t + m + 1)
                        nc.scalar.activation(c_g[:, m], gate(C, m, par, v), ACT.Tanh).then_inc(c_ready, 1)
                    if v == 1 and not last:
                        seed(C, 1 - par)
                    if v % 2 and not (first and v < 2):
                        copy_pair(2 * grp + v // 2 - 1)

            groups(act, group)
            copy_pair(T // 2 - 1)

        @block.vector
        def _(dve):
            def per_column(v, n):
                return v.rearrange("p (c u) -> p c u", u=1).broadcast_to([P, v.shape[1], n])

            nc.vector.memset(zeros[:], 0.0)
            dve.wait_ge(pe_prep, 1)
            nc.vector.tensor_copy(condT[:].rearrange("p k b -> p (k b)"),
                                  ps[:, 0, 0:KC * B]).then_inc(dve_prep, 1)
            nc.vector.tensor_copy(bias[:], ps[:, 0, 256:256 + BIAS_ROWS]).then_inc(dve_prep, 1)
            dve.wait_ge(dve_prep, 2)
            nc.vector.tensor_tensor(kv_off[:], bias[:, BKV:BKV + 4], bias[:, NK:NK + 4],
                                    ALU.subtract).then_inc(dve_prep, 1)
            dve.wait_ge(dve_prep, 3)
            dve.wait_ge(pe_prep, 3)
            nc.vector.tensor_tensor(dkv[:], ps[:, 2, 0:4 * B].rearrange("p (o b) -> p o b", o=4),
                                    per_column(kv_off[:], B), ALU.add).then_inc(dve_prep, 1)
            dve.wait_ge(dve_prep, 4)
            for first in (0, 2):
                for o in (first, first + 1):
                    i = nc.vector.tensor_tensor(
                        blk[:, o], per_column(dkv[:, o], HALF),
                        head_mask.rearrange("p (u h) -> p u h", u=1).broadcast_to([P, B, HALF]), ALU.mult)
                i.then_inc(dve_prep, 1)
            dve.wait_ge(pe_prep, 4)
            nc.vector.tensor_copy(s_off[:], ps[:, 3, 8:8 + G])
            nc.vector.tensor_tensor(x_off[:], ps[:, 3, 0:KC], bias[:, BP:BP + KC],
                                    ALU.add).then_inc(dve_prep, 1)
            dve.wait_ge(pe_prep, 8)
            for j in range(2):
                i = nc.vector.tensor_copy(dq[:, 1, :, j, :], ps[:, 6 + j].rearrange("p (g n) -> p g n", g=G))
            i.then_inc(dve_prep, 1)
            for n in range(2):
                dve.wait_ge(pe_prep, 11 + n)
                nc.vector.tensor_copy(nproj[:, 4 + 2 * n:6 + 2 * n, :].rearrange("p g e -> p (g e)"),
                                      ps[:, 2 + n, :]).then_inc(dve_prep, 1)
            dve.wait_ge(dve_prep, 10)

            def turned(s, q):
                dve.wait_ge(turn_ready, 4 * s + q + 1)
                nc.vector.tensor_copy(
                    xT[:, :, bass.ds(s * TS + 4 * q, 4), :].rearrange("p k t b -> p k (t b)"),
                    ps[:, 1].rearrange("p (k n) -> p k n", k=KC)).then_inc(xT_dve, 1)

            def mask(s, gh):
                dve.wait_ge(w1_ready, G * s + 4 * gh + 4)
                nc.vector.tensor_tensor(
                    w1m[:, 4 * gh:4 * gh + 4].rearrange("p g (t b) -> p (g t) b", b=GB),
                    w1[:, 4 * gh:4 * gh + 4].rearrange("p g (t b) -> p (g t) b", b=GB),
                    batch_mask.rearrange("p (u b) -> p u b", u=1).broadcast_to([P, 4 * TS, GB]),
                    ALU.mult).then_inc(w1m_ready, 1)

            def block_of(s, gh, m):
                return slice(None), m, bass.ds(s * TS, TS), slice(4 * GB * gh, 4 * GB * (gh + 1))

            def residual(s):
                for gh in range(2):
                    for m in range(KC):
                        dve.wait_ge(attn_ready, 4 * s + 2 * gh + m + 1)
                        cols = xT[block_of(s, gh, m)]
                        nc.vector.scalar_tensor_tensor(
                            out=cols, in0=ps[:, 4 + 2 * gh + m].rearrange("p (t c) -> p t c", t=TS),
                            scalar=x_off[:, m:m + 1], in1=cols,
                            op0=ALU.add, op1=ALU.add).then_inc(x1_ready, 1)
                for gh in range(2):
                    for m in range(KC):
                        dve.wait_ge(x_hi_ready, 4 * s + 2 * gh + m + 1)
                        at = block_of(s, gh, m)
                        nc.vector.tensor_tensor(x_lo[at], xT[at], x_hi[at].bitcast(F32),
                                                ALU.subtract).then_inc(x_lo_ready, 1)

            for q in (1, 3):
                turned(0, q)
            with dve.Fori(0, SLICES - 1) as s:
                for gh in range(2):
                    turned(s + 1, 2 * gh + 1)
                    mask(s, gh)
                residual(s)
            for gh in range(2):
                mask(SLICES - 1, gh)
            residual(SLICES - 1)

            dve.wait_ge(pe_prep, 13)
            nc.vector.tensor_tensor(
                vcond[:].rearrange("p g k b -> p (g k) b"),
                ps[:, 7, 0:6 * B].rearrange("p (o b) -> p o b", o=6),
                per_column(bias[:, BZ:BZ + 6], B), ALU.add).then_inc(v_ready, 1)
            nc.vector.memset(h[:, 1], 0.0).then_inc(h_ready, 2)
            nc.vector.memset(h_rest[:], 0.0).then_inc(h_rest_ready, 2)
            nc.vector.memset(h_last[:], 0.0).then_inc(h_last_ready, 2)

            def parts(whole, ready, rest, rest_ready, last, last_ready, n):
                for k in range(KC):
                    dve.wait_ge(ready, n + k + 1)
                    nc.vector.tensor_tensor(rest[:, k], whole[:, k], top(whole[:, k]),
                                            ALU.subtract).then_inc(rest_ready, 1)
                for k in range(KC):
                    dve.wait_ge(rest_ready, n + k + 1)
                    nc.vector.tensor_tensor(last[:, k], rest[:, k], top(rest[:, k]),
                                            ALU.subtract).then_inc(last_ready, 1)

            def group(grp, par, first=False, last=False):
                for v in range(GS):
                    t = GS * grp + v
                    now, prev = h[:, v % 2], h[:, (v + 1) % 2]
                    for k in range(KC):
                        dve.wait_ge(r_ready, 2 * t + k + 1)
                        nc.vector.tensor_tensor(rh[:, k], r_g[:, k], prev[:, k], ALU.mult).then_inc(rh_ready, 1)
                    parts(rh, rh_ready, rh_rest, rh_rest_ready, rh_last, rh_last_ready, 2 * t)
                    dve.wait_ge(z_ready, t + 1)
                    nc.vector.scalar_tensor_tensor(out=keep[:], in0=z_g[:], scalar=1.0, in1=prev,
                                                   op0=ALU.subtract, op1=ALU.mult).then_inc(keep_ready, 1)
                    for k in range(KC):
                        dve.wait_ge(c_ready, 2 * t + k + 1)
                        nc.vector.tensor_tensor(zc[:, k], z_g[:, k], c_g[:, k], ALU.mult).then_inc(zc_ready, 1)
                    dve.wait_ge(keep_ready, t + 1)
                    if not (first and v < 2):
                        dve.wait_ge(y_ready, t - 1)
                    for k in range(KC):
                        dve.wait_ge(zc_ready, 2 * t + k + 1)
                        nc.vector.tensor_tensor(now[:, k], zc[:, k], keep[:, k],
                                                ALU.subtract).then_inc(h_ready, 1)
                    if not (last and v == GS - 1):
                        parts(now, h_ready, h_rest, h_rest_ready, h_last, h_last_ready, 2 * t + 2)

            groups(dve, group)

        @block.gpsimd
        def _(pool):
            tt, copy = nc.gpsimd.tensor_tensor, nc.gpsimd.tensor_copy
            done = [0]

            def after(i):
                i.then_inc(split, 1)
                done[0] += 1
                pool.wait_ge(split, done[0])

            pool.wait_ge(gru_in, 16 * 9)
            for g in (R, Z, C):
                after(copy(w_hi[g][:], w_in[g][:]))
                tt(w_lo[g][:], w_in[g][:], w_hi[g][:].bitcast(F32), ALU.subtract).then_inc(w_split, 1)
            for g in (R, Z, C):
                for n in range(2):
                    after(copy(u_part[g][n][:], w_rec[g][:]))
                    after(tt(w_rec[g][:], w_rec[g][:], u_part[g][n][:], ALU.subtract))
                copy(u_part[g][2][:], w_rec[g][:]).then_inc(w_split, 1)

            def group(grp, par, first=False, last=False):
                for v in range(GS):
                    t = GS * grp + v
                    slot = v // 2
                    pool.wait_ge(h_ready, 2 * t + 4)
                    if v % 2 == 0 and not (first):
                        pool.wait_ge(yT_ready, 2 * grp + slot - 1)
                    tt(y[:, slot, :, v % 2], xT[:, :, bass.ds(t, 1), :].rearrange("p k t b -> p k (t b)"),
                       h[:, v % 2], ALU.add).then_inc(y_ready, 1)

            groups(pool, group)


_INS = ["x", "cond_1024", "L0_cond_W_q", "L0_cond_b_q", "L0_cond_W_kv", "L0_cond_b_kv",
        "L0_cond_no_op_k", "L0_cond_no_op_v", "L0_cond_W_proj", "L0_cond_b_proj",
        "L1_cond_W_z", "L1_cond_U_z", "L1_cond_C_z", "L1_cond_b_z",
        "L1_cond_W_r", "L1_cond_U_r", "L1_cond_C_r", "L1_cond_b_r",
        "L1_cond_W", "L1_cond_U", "L1_cond_C", "L1_cond_b"]
_ROWS = {"b_q", "b_kv", "no_op_k", "no_op_v", "b_proj", "b_z", "b_r", "b"}


def kernel(**inputs):
    import numpy as np
    import concourse.bacc as bacc
    from concourse.bass_utils import run_bass_kernel_spmd

    nc = bacc.Bacc("TRN2", target_bir_lowering=False, num_devices=1)
    arrays, args = {}, []

    def give(name, a):
        a = np.ascontiguousarray(a)
        arrays[name] = a
        return nc.dram_tensor(name, a.shape, mybir.dt.from_np(a.dtype), kind="ExternalInput").ap()

    p = np.arange(P)
    consts = np.concatenate([np.eye(P), p[:, None] // 16 == np.arange(HALF),
                             p[:, None] // HALF % GB == np.arange(GB)], axis=1).astype(np.float32)
    for name in _INS:
        a = np.asarray(inputs[name])
        if name.split("cond_", 1)[-1] in _ROWS:
            a = a.reshape(-1, P)
        args.append(give("in_" + name, a))
        if name == "cond_1024":
            args.append(give("in_consts", consts))
    shape = np.asarray(inputs["x"]).shape
    args.append(nc.dram_tensor("out_0", shape, F32, kind="ExternalOutput").ap())
    build(nc, *args)
    r = run_bass_kernel_spmd(nc, [arrays], core_ids=[0])
    return r.results[0]["out_0"]
```

```python
from contextlib import ExitStack

import concourse.bass as bass
from concourse import mybir

F32 = mybir.dt.float32
F32R = mybir.dt.float32r
F16 = mybir.dt.float16
I32 = mybir.dt.int32
BF16 = mybir.dt.bfloat16
ALU = mybir.AluOpType
ACT = mybir.ActivationFunctionType

P = 128
HEADS = 16
HALF = 8
GB = 8
TS = 16
GS = 4
BQ, NK, NV, BKV, BP, BZ, BR, BC = 0, 2, 4, 6, 10, 12, 14, 16
VECTORS = 18
H_SCALE = 2.0 ** 10
U_TOP = 2.0 ** 14
WARM_UP = 10
Z, R, C = 0, 1, 2


def build(nc, x, condT_vectors, consts, W_qT, W_kv, W_proj, W_z, U_z, C_z, W_r, U_r, C_r, W, U, C_, out):
    B, T, D = x.shape
    KC = D // P
    G = B // GB
    SLICES = T // TS
    PAIRS = TS // 2
    HD = D // HEADS
    assert B == 64 and KC == 2 and HD * HALF == P and GB * HEADS == P and G == 8

    with ExitStack() as ctx:
        def sb(name, shape, dt=F32):
            return ctx.enter_context(nc.sbuf_tensor(name, shape, dt))

        def sem(name):
            return ctx.enter_context(nc.semaphore(name))

        ps = ctx.enter_context(nc.psum_tensor("ps", [P, 8, 512], F32))

        cst = sb("cst", [P, P + HALF + GB])
        ident = cst[:, 0:P]
        head_mask = cst[:, P:P + HALF]
        batch_mask = cst[:, P + HALF:]
        small = sb("small", [P, KC * B + VECTORS])
        condT = small[:, 0:KC * B].rearrange("p (k b) -> p k b", k=KC)
        bias = small[:, KC * B:]
        wqT = sb("wqT", [P, 2, D])
        wkv = sb("wkv", [P, KC, 2 * D])
        wp = sb("wp", [P, KC, D])
        w_in = [sb(f"w_in{g}", [P, KC, D]) for g in range(3)]
        w_rec = [sb(f"w_rec{g}", [P, KC, D]) for g in range(3)]
        w_hi = [sb(f"w_hi{g}", [P, KC, D], F32R) for g in range(3)]
        w_lo = [sb(f"w_lo{g}", [P, KC, D], F32R) for g in range(3)]
        u_part = {g: [sb(f"u{g}_{n}", [P, KC, D], F16 if g == Z else BF16) for n in range(2 if g == Z else 3)]
                  for g in (Z, R, C)}
        w_cond = [sb(f"w_cond{g}", [P, KC, D]) for g in range(3)]
        xn = sb("xn", [P, 2, PAIRS, D])

        kv_off = sb("kv_off", [P, 4])
        dkv = sb("dkv", [P, 4, B])
        blk = sb("blk", [P, 4, B, HALF])
        dq = sb("dq", [P, KC, G, 2, GB * HALF])
        s_off = sb("s_off", [P, G])
        nproj = sb("nproj", [P, G, D])
        x_off = sb("x_off", [P, KC])
        vcond = sb("vcond", [P, 3, KC, B])
        zeros = sb("zeros", [P, 512], BF16)

        xT = sb("xT", [P, KC, T, B])
        turned_back = sb("turned_back", [P, T // 2, D])
        x_hi = sb("x_hi", [P, 2, KC, GS * B], F32R)
        x_lo = sb("x_lo", [P, 2, KC, GS * B], F32R)
        w1 = sb("w1", [P, G, TS * GB])
        w1m = sb("w1m", [P, G, TS * GB])
        hs = sb("hs", [P, 2, KC, B])
        h16 = [sb(f"h16_{n}", [P, KC, B], F16) for n in range(2)]
        r_g = sb("r_g", [P, KC, B])
        z_g = sb("z_g", [P, KC, B])
        c_g = sb("c_g", [P, KC, B])
        rh = sb("rh", [P, KC, B])
        rh16 = [sb(f"rh16_{n}", [P, KC, B], F16) for n in range(2)]
        u_max = sb("u_max", [P, 1])
        u_top = sb("u_top", [P, 1])
        u_pow = sb("u_pow", [P, 1])
        u_scale = sb("u_scale", [P, 1])
        scale = sb("scale", [P, 1])
        unscale = sb("unscale", [P, 1])
        keep = sb("keep", [P, KC, B])
        zc = sb("zc", [P, KC, B])
        y = sb("y", [P, 2, KC, 2, B])

        small_in = sem("small_in")
        wkv_in = [sem("wk_in"), sem("wv_in")]
        attn_in = sem("attn_in")
        x_in = [sem(f"x_in{s}") for s in range(SLICES)]
        gate_in = [sem("gate_in_z"), sem("gate_in_r"), sem("gate_in_c")]
        uz_in = sem("uz_in")
        cond_w_in = sem("cond_w_in")
        out_done = sem("out_done")
        blk_ready = sem("blk_ready")
        kv_ready = sem("kv_ready")
        pe_prep = sem("pe_prep")
        act_prep = sem("act_prep")
        dve_prep = sem("dve_prep")
        turn_ready = sem("turn_ready")
        xT_act = sem("xT_act")
        xT_dve = sem("xT_dve")
        score_ready = sem("score_ready")
        w1_ready = sem("w1_ready")
        w1m_ready = sem("w1m_ready")
        attn_ready = sem("attn_ready")
        x1_ready = sem("x1_ready")
        zeros_ready = sem("zeros_ready")
        v_made = sem("v_made")
        v_ready = sem("v_ready")
        seeded = [sem("seeded_z"), sem("seeded_r"), sem("seeded_c")]
        hs_ready = sem("hs_ready")
        h16_ready = [[sem(f"h16_{n}_ready{k}") for k in range(KC)] for n in range(2)]
        r_pre = [sem(f"r_pre{k}") for k in range(KC)]
        z_pre = [sem(f"z_pre{k}") for k in range(KC)]
        c_pre = [sem(f"c_pre{k}") for k in range(KC)]
        r_ready = [sem(f"r_ready{k}") for k in range(KC)]
        z_ready = sem("z_ready")
        c_ready = [sem(f"c_ready{k}") for k in range(KC)]
        rh_ready = sem("rh_ready")
        rh16_ready = [[sem(f"rh16_{n}_ready{k}") for k in range(KC)] for n in range(2)]
        x_used = sem("x_used")
        u_max_ready = sem("u_max_ready")
        u_top_ready = sem("u_top_ready")
        scale_ready = sem("scale_ready")
        x_hi_ready = sem("x_hi_ready")
        x_lo_ready = sem("x_lo_ready")
        split = sem("split")
        w_split = sem("w_split")
        zc_ready = [sem(f"zc_ready{k}") for k in range(KC)]
        y_ready = sem("y_ready")
        yT_ready = sem("yT_ready")
        o_ready = sem("o_ready")

        GATE_BANK = {Z: 2, C: 4, R: 6}
        YT_BANK = 0
        GROUPS = T // GS
        assert GROUPS % 2 == 0 and GROUPS >= 4

        def gate(g, m, par, v, n=1):
            at = (par * GS + v) * B
            return ps[:, GATE_BANK[g] + m, at:at + n * B]

        def gate_both(g, par, v, n=1):
            at = (par * GS + v) * B
            return ps[:, GATE_BANK[g]:GATE_BANK[g] + KC, at:at + n * B]

        def x1_of(grp, k):
            return xT[:, k, bass.ds(grp * GS, GS), :].rearrange("p t b -> p (t b)")

        N_BANK = (4, 5, 2, 3)

        def n_blocks(n):
            for g in range(2):
                for j in range(2):
                    yield (nproj[j * 64:(j + 1) * 64, 2 * n + g, :],
                           ps[g * 64:(g + 1) * 64, N_BANK[n], j * D:(j + 1) * D])

        def value(eng, v):
            return v if isinstance(v, int) else eng.snap(v)

        def groups(eng, body):
            body(0, 0, first=True)
            with eng.Fori(0, GROUPS // 2 - 1) as i:
                body(2 * i + 1, 1)
                body(2 * i + 2, 0)
            body(GROUPS - 1, 1, last=True)

        block = ctx.enter_context(nc.Block())

        @block.sync
        def _(sp):
            def weights(src, dst, arrived):
                sp.dma_start(dst[:], src.rearrange("(k p) n -> p k n", p=P)).then_inc(arrived, 16)

            def load_x(s):
                for q in range(2):
                    src = x[:, s * TS:(s + 1) * TS, :].rearrange("b (i q) d -> q b i d", q=2)[q]
                    sp.dma_start(xn[q * B:(q + 1) * B, s % 2], src).then_inc(x_in[s], 16)

            sp.dma_start(small[:], condT_vectors).then_inc(small_in, 16)
            sp.dma_start(cst[:], consts).then_inc(small_in, 16)
            for g, w in ((R, C_r), (Z, C_z), (C, C_)):
                weights(w, w_cond[g], cond_w_in)
            weights(W_qT, wqT, attn_in)
            weights(W_proj, wp, attn_in)
            weights(U_z, w_rec[Z], uz_in)
            load_x(0)
            for g, w, u in ((R, W_r, U_r), (C, W, U)):
                weights(w, w_in[g], gate_in[g])
                weights(u, w_rec[g], gate_in[g])
            load_x(1)
            weights(W_z, w_in[Z], gate_in[Z])
            for s in range(2, SLICES):
                sp.wait_ge(turn_ready, 4 * (s - 1))
                load_x(s)
            with sp.Fori(0, T // 2) as pair:
                sp.wait_ge(o_ready, pair + 1)
                dst = out.rearrange("b (i q) d -> q b i d", q=2)[:, :, bass.ds(pair, 1)]
                sp.dma_start(dst.rearrange("q b i d -> q b (i d)"),
                             turned_back[:, bass.ds(pair, 1), :].rearrange("p i d -> p (i d)")
                             ).then_inc(out_done, 16)
            sp.wait_ge(out_done, 16 * T // 2)

        @block.tensor
        def _(pe):
            mm = nc.tensor.matmul

            pe.wait_ge(zeros_ready, 1)
            for _ in range(WARM_UP):
                mm(ps[:, 2, :], zeros[:, 0:P], zeros[:], start=True, stop=True)
            pe.wait_ge(small_in, 16 * 2)
            for o in range(4):
                if o % 2 == 0:
                    pe.wait_ge(wkv_in[o // 2], 16)
                for k in range(KC):
                    i = mm(ps[:, o // 2, (o % 2) * B:(o % 2 + 1) * B], wkv[:, k, o * P:(o + 1) * P], condT[:, k, :],
                           start=(k == 0), stop=(k == KC - 1))
                if o % 2:
                    i.then_inc(kv_ready, 1)
            pe.wait_ge(cond_w_in, 16 * 3)
            for g in range(3):
                for m in range(KC):
                    for k in range(KC):
                        i = mm(ps[:, 2, (g * KC + m) * B:(g * KC + m + 1) * B],
                               w_cond[g][:, k, m * P:(m + 1) * P], condT[:, k, :],
                               start=(k == 0), stop=(k == KC - 1))
            i.then_inc(v_made, 1)
            pe.wait_ge(attn_in, 16 * 2)
            for j in range(2):
                pe.wait_ge(blk_ready, j + 1)
                for k in range(KC):
                    for n in range(2):
                        i = mm(ps[:, 4 + 2 * k + j, n * 256:(n + 1) * 256], wqT[:, j, k * P:(k + 1) * P],
                               blk[:, j, n * B // 2:(n + 1) * B // 2, :], start=True, stop=True)
                    i.then_inc(pe_prep, 1)
                    if k == 0:
                        for jj in range(2):
                            mm(ps[:, 3, j:j + 1], wp[:, jj, j * P:(j + 1) * P], bias[:, NV + jj:NV + jj + 1],
                               start=(jj == 0), stop=(jj == 1))
                        for g in range(G):
                            mm(ps[j * 64:(j + 1) * 64, 3, 8 + g:9 + g], blk[:, j, g * GB:(g + 1) * GB, :],
                               bias[:, BQ + j:BQ + j + 1], start=True, stop=True)

            def n_products(n):
                for j in range(2):
                    i = mm(ps[:, N_BANK[n], j * D:(j + 1) * D], blk[:, 2 + j, 2 * n * GB:2 * (n + 1) * GB, :],
                           wp[:, j, :], start=True, stop=True)
                i.then_inc(pe_prep, 1)

            def turn(s, half):
                pe.wait_ge(x_in[s], 32)
                for q in (2 * half, 2 * half + 1):
                    if q == 0 and s == 0:
                        pe.wait_ge(dve_prep, 3)
                    elif q % 2 == 0:
                        pe.wait_ge(xT_act, 2 * s + half)
                    elif 2 * s + half:
                        pe.wait_ge(xT_dve, 2 * s + half)
                    for k in range(KC):
                        for p in range(2):
                            i = nc.tensor.transpose(
                                ps[:, q % 2, k * 256 + p * P:k * 256 + (p + 1) * P],
                                xn[:, s % 2, 2 * q + p, k * P:(k + 1) * P], ident)
                    i.then_inc(turn_ready, 1)

            turn(0, 0)
            pe.wait_ge(blk_ready, 4)
            pe.wait_ge(v_ready, 1)
            n_products(2)
            pe.wait_ge(dve_prep, 4)
            n_products(3)
            turn(0, 1)
            pe.wait_ge(act_prep, 1)
            for n in range(2):
                n_products(n)
            pe.wait_ge(act_prep, 2)
            for s in range(SLICES):
                pe.wait_ge(xT_act, 2 * s + 2)
                pe.wait_ge(xT_dve, 2 * s + 2)
                if s:
                    pe.wait_ge(w1_ready, G * s)
                for g in range(G):
                    if s == 0 and g == 4:
                        pe.wait_ge(dve_prep, 6)
                    for k in range(KC):
                        i = mm(ps[:, 2 + g // 4, (g % 4) * P:(g % 4 + 1) * P], dq[:, k, g],
                               xT[:, k, s * TS:(s + 1) * TS, g * GB:(g + 1) * GB],
                               start=(g % 4 == 0 and k == 0), stop=(k == KC - 1), skip_group_check=True)
                    if g % 4 == 3:
                        i.then_inc(score_ready, 1)
                for gh in range(2):
                    if s < SLICES - 1:
                        turn(s + 1, gh)
                    pe.wait_ge(w1m_ready, 2 * s + gh + 1)
                    for m in range(KC):
                        if gh == 0 and m == 0 and s == 0:
                            pe.wait_ge(act_prep, 4)
                        if gh == 0 and m == 0 and s:
                            pe.wait_ge(x1_ready, 4 * s)
                        bank = ps[:, 4 + gh * 2 + m].rearrange("p (t c) -> p t c", c=4 * GB)
                        for gl in range(4):
                            i = mm(bank[:, :, gl * GB:(gl + 1) * GB],
                                   nproj[:, gh * 4 + gl, m * P:(m + 1) * P], w1m[:, gh * 4 + gl],
                                   start=(gl == 0), stop=True, skip_group_check=True)
                        i.then_inc(attn_ready, 1)

            def add(dst, lhsT, rhs):
                return mm(dst, lhsT, rhs, start=False, stop=False, skip_group_check=True)

            PASSES = [(m, k, n) for ns in ((0, 1), (2,)) for m in range(KC) for k in range(KC) for n in ns]
            C_PASSES = [(1, 0, 0), (1, 0, 1), (0, 0, 0), (0, 0, 1), (0, 0, 2), (1, 0, 2),
                        (1, 1, 0), (0, 1, 0), (0, 1, 1), (0, 1, 2), (1, 1, 1), (1, 1, 2)]
            assert sorted(C_PASSES) == sorted(PASSES)

            def passes(g, which):
                return (C_PASSES if g == C else PASSES)[which]

            def project(g, which, par):
                for m, k, n in passes(g, which):
                    w, xp = ((w_hi, x_hi), (w_lo, x_hi), (w_hi, x_lo))[n]
                    i = add(gate(g, m, par, 0, GS), w[g][:, k, m * P:(m + 1) * P], xp[:, par, k])
                return i

            def recur(g, par, v, n, blocks, parts, ready, one_more, done=None):
                for m in range(KC):
                    for k in blocks:
                        if m == 0:
                            pe.wait_ge(ready[n][k], one_more)
                        for w in range(len(u_part[g]) - n):
                            i = add(gate(g, m, par, v), u_part[g][w][:, k, m * P:(m + 1) * P], parts[n][:, k])
                    if done:
                        i.then_inc(done[m], 1)

            WHILE_RH = [None, slice(0, 2), slice(5, 7), slice(10, 12)]
            WHILE_H = [((R, slice(0, 8)),),
                       ((R, slice(8, 12)), (Z, slice(0, 1)), (C, slice(2, 5))),
                       ((Z, slice(1, 6)), (C, slice(7, 10))),
                       ((Z, slice(6, 12)),)]

            def group(grp, par, first=False, last=False):
                for v in range(GS):
                    one_more = value(pe, GS * grp + v + 1)
                    if not (first and v == 0):
                        recur(R, par, v, 0, (0,), h16, h16_ready, one_more)
                        if v == 1 and not last:
                            pe.wait_ge(seeded[Z], grp + 2)
                        recur(Z, par, v, 0, (0,), h16, h16_ready, one_more)
                        recur(R, par, v, 0, (1,), h16, h16_ready, one_more)
                        recur(R, par, v, 1, (0, 1), h16, h16_ready, one_more, r_pre)
                        recur(Z, par, v, 0, (1,), h16, h16_ready, one_more)
                        recur(Z, par, v, 1, (0, 1), h16, h16_ready, one_more, z_pre)
                    if not (first and v < 2):
                        pair = 2 * grp + v // 2 - 1
                        if v % 2 == 0:
                            pe.wait_ge(y_ready, 2 * pair + 2)
                            if not first:
                                pe.wait_ge(o_ready, pair)
                        i = nc.tensor.transpose(ps[:, YT_BANK, (v % 2) * P:(v % 2 + 1) * P],
                                                y[:, (v // 2 + 1) % 2, v % 2].rearrange("p t b -> p (t b)"), ident)
                        if v % 2:
                            i.then_inc(yT_ready, 1)
                    if WHILE_RH[v] and not last:
                        project(C, WHILE_RH[v], 1 - par)
                    if not (first and v == 0):
                        if v == 0:
                            pe.wait_ge(seeded[C], grp + 2)
                        recur(C, par, v, 0, (0,), rh16, rh16_ready, one_more)
                        recur(C, par, v, 0, (1,), rh16, rh16_ready, one_more)
                        recur(C, par, v, 1, (0, 1), rh16, rh16_ready, one_more, c_pre)
                    if not last:
                        if v == GS - 1:
                            pe.wait_ge(seeded[R], grp + 3)
                        for g, which in WHILE_H[v]:
                            if v == 0:
                                pe.wait_ge(x_hi_ready, KC * (grp + 2))
                            if v == 1 and g == R:
                                pe.wait_ge(x_lo_ready, KC * (grp + 2))
                            if g == Z:
                                pe.wait_ge(z_ready, one_more)
                            if g == C:
                                pe.wait_ge(c_ready[max(m for m, k, n in passes(g, which))], one_more)
                            i = project(g, which, 1 - par)
                        if v == GS - 1:
                            i.then_inc(x_used, 1)

            pe.wait_ge(x_lo_ready, 2 * KC)
            pe.wait_ge(w_split, 6)
            pe.wait_ge(seeded[Z], 1)
            project(Z, slice(0, 12), 0).then_inc(z_pre[KC - 1], 1)
            pe.wait_ge(seeded[C], 2)
            project(C, slice(0, 10), 0).then_inc(c_pre[0], 1)
            project(C, slice(10, 12), 0).then_inc(c_pre[1], 1)
            pe.wait_ge(seeded[R], 2)
            project(R, slice(0, 12), 0).then_inc(x_used, 1)
            groups(pe, group)
            pe.wait_ge(y_ready, T)
            pe.wait_ge(o_ready, T // 2 - 1)
            for k in range(KC):
                i = nc.tensor.transpose(ps[:, YT_BANK, k * P:(k + 1) * P],
                                        y[:, 1, k].rearrange("p t b -> p (t b)"), ident)
            i.then_inc(yT_ready, 1)

        @block.scalar
        def _(act):
            for n, cols in enumerate((slice(0, D), slice(D, 2 * D))):
                act.dma_start(wkv[:, :, cols], W_kv.rearrange("(k p) n -> p k n", p=P)[:, :, cols]
                              ).then_inc(wkv_in[n], 16)
            nc.scalar.preload_act_table(ACT.Sigmoid)
            act.wait_ge(pe_prep, 3)
            nc.scalar.copy(dq[:, 0, :, 0, :], ps[:, 4].rearrange("p (g n) -> p g n", g=G))
            nc.scalar.copy(dq[:, 0, :, 1, :], ps[:, 5].rearrange("p (g n) -> p g n", g=G)).then_inc(act_prep, 1)

            def n_copy(n, made):
                act.wait_ge(pe_prep, made)
                for dst, src in n_blocks(n):
                    i = nc.scalar.copy(dst, src)
                i.then_inc(act_prep, 1)

            def turned(s, which=(0, 2)):
                for q in which:
                    act.wait_ge(turn_ready, 4 * s + q + 1)
                    nc.scalar.copy(
                        xT[:, :, bass.ds(s * TS + 4 * q, 4), :].rearrange("p k t b -> p k (t b)"),
                        ps[:, 0].rearrange("p (k n) -> p k n", k=KC)).then_inc(xT_act, 1)

            def softmax(s, gh):
                for g in range(4 * gh, 4 * gh + 4):
                    if g % 4 == 0:
                        act.wait_ge(score_ready, 2 * s + g // 4 + 1)
                    nc.scalar.activation(w1[:, g], ps[:, 2 + g // 4, (g % 4) * P:(g % 4 + 1) * P],
                                         ACT.Sigmoid, bias=s_off[:, g:g + 1]).then_inc(w1_ready, 1)

            def round_x1(grp, par, k):
                nc.scalar.copy(x_hi[:, par, k], x1_of(grp, k)).then_inc(x_hi_ready, 1)

            turned(0, (0,))
            n_copy(2, 5)
            turned(0, (2,))
            for n in range(2):
                n_copy(n, 7 + n)
            act.wait_ge(dve_prep, 4)
            with act.Fori(0, SLICES - 1) as s:
                softmax(s, 0)
                softmax(s, 1)
                turned(s + 1)
            act.wait_ge(x1_ready, 4)
            for grp in range(2):
                for k in range(KC):
                    round_x1(grp, grp, k)
            softmax(SLICES - 1, 0)
            softmax(SLICES - 1, 1)

            def seed(g, par):
                nc.scalar.copy(
                    gate_both(g, par, 0, GS).rearrange("p k (t b) -> p k t b", t=GS),
                    vcond[:, g].rearrange("p k (u b) -> p k u b", u=1).broadcast_to([P, KC, GS, B])
                ).then_inc(seeded[g], 1)

            act.wait_ge(v_ready, 2)
            act.wait_ge(w1_ready, G * SLICES)
            seed(Z, 0)
            act.wait_ge(x1_ready, 4 * (SLICES - 1) + 2)
            for par in range(2):
                seed(C, par)

            def copy_pair(pair):
                act.wait_ge(yT_ready, pair + 1)
                nc.scalar.copy(turned_back[:, bass.ds(pair, 1), :].rearrange("p i d -> p (i d)"),
                               ps[:, YT_BANK, 0:D]).then_inc(o_ready, 1)

            def group(grp, par, first=False, last=False):
                for v in range(GS):
                    one_more = value(act, GS * grp + v + 1)
                    if v == 0 and not (first or last):
                        act.wait_ge(x_used, grp)
                        round_x1(grp + 1, 1 - par, 0)
                    if not (first and v == 0):
                        for m in range(KC):
                            act.wait_ge(r_pre[m], one_more)
                            nc.scalar.activation(r_g[:, m], gate(R, m, par, v), ACT.Sigmoid,
                                                 scale=1 / H_SCALE).then_inc(r_ready[m], 1)
                    if v == 0 and not (first or last):
                        round_x1(grp + 1, 1 - par, 1)
                    act.wait_ge(z_pre[KC - 1], one_more)
                    nc.scalar.activation(z_g[:], gate_both(Z, par, v), ACT.Sigmoid,
                                         scale=unscale[:, 0:1]).then_inc(z_ready, 1)
                    if first and v == 0:
                        act.wait_ge(x1_ready, 4 * SLICES)
                        for slots in range(2):
                            seed(R, slots)
                    if v == GS - 1 and not last:
                        act.wait_ge(r_ready[KC - 1], one_more)
                        seed(R, par)
                    for m in range(KC):
                        act.wait_ge(c_pre[m], one_more)
                        nc.scalar.activation(c_g[:, m], gate(C, m, par, v), ACT.Tanh,
                                             scale=1 / H_SCALE).then_inc(c_ready[m], 1)
                    if v == 0 and not last:
                        seed(Z, 1 - par)
                    if v == GS - 1 and not last:
                        act.wait_ge(c_ready[KC - 1], one_more)
                        seed(C, par)
                    if v % 2 and not (first and v < 2):
                        copy_pair(2 * grp + v // 2 - 1)

            groups(act, group)
            copy_pair(T // 2 - 1)

        @block.vector
        def _(dve):
            def per_column(v, n):
                return v.rearrange("p (c u) -> p c u", u=1).broadcast_to([P, v.shape[1], n])

            nc.vector.memset(zeros[:], 0.0).then_inc(zeros_ready, 1)
            nc.vector.memset(hs[:, 1], 0.0).then_inc(hs_ready, 1)
            dve.sem_inc(rh_ready, 1)
            for k in range(KC):
                dve.sem_inc(r_pre[k], 1)
                dve.sem_inc(r_ready[k], 1)
                for n in range(2):
                    dve.sem_inc(h16_ready[n][k], 1)
                    dve.sem_inc(rh16_ready[n][k], 1)

            dve.wait_ge(small_in, 16 * 2)
            nc.vector.tensor_tensor(kv_off[:], bias[:, BKV:BKV + 4], bias[:, NK:NK + 4],
                                    ALU.subtract).then_inc(dve_prep, 1)
            dve.wait_ge(dve_prep, 1)
            for n, rows in enumerate((slice(0, 2), slice(2, 4))):
                dve.wait_ge(kv_ready, n + 1)
                nc.vector.tensor_tensor(dkv[:, rows], ps[:, n, 0:2 * B].rearrange("p (o b) -> p o b", o=2),
                                        per_column(kv_off[:, rows], B), ALU.add).then_inc(dve_prep, 1)
                dve.wait_ge(dve_prep, 2 + n)
                for o in (2 * n, 2 * n + 1):
                    nc.vector.tensor_tensor(
                        blk[:, o], per_column(dkv[:, o], HALF),
                        head_mask.rearrange("p (u h) -> p u h", u=1).broadcast_to([P, B, HALF]),
                        ALU.mult).then_inc(blk_ready, 1)
            dve.wait_ge(v_made, 1)
            nc.vector.tensor_tensor(
                vcond[:].rearrange("p g k b -> p (g k) b"),
                ps[:, 2, 0:6 * B].rearrange("p (o b) -> p o b", o=6),
                per_column(bias[:, BZ:BZ + 6], B), ALU.add).then_inc(v_ready, 1)
            dve.wait_ge(uz_in, 16)
            nc.vector.tensor_reduce(u_max[:], w_rec[Z][:].rearrange("p k n -> p (k n)"), mybir.AxisListType.X,
                                    ALU.max, apply_absolute_value=True).then_inc(u_max_ready, 1)
            dve.wait_ge(pe_prep, 4)
            nc.vector.tensor_copy(s_off[:], ps[:, 3, 8:8 + G])
            nc.vector.tensor_tensor(x_off[:], ps[:, 3, 0:KC], bias[:, BP:BP + KC],
                                    ALU.add).then_inc(dve_prep, 1)
            for j in range(2):
                i = nc.vector.tensor_copy(dq[:, 1, :, j, :], ps[:, 6 + j].rearrange("p (g n) -> p g n", g=G))
            i.then_inc(dve_prep, 1)

            def turned(s, q):
                dve.wait_ge(turn_ready, 4 * s + q + 1)
                nc.vector.tensor_copy(
                    xT[:, :, bass.ds(s * TS + 4 * q, 4), :].rearrange("p k t b -> p k (t b)"),
                    ps[:, 1].rearrange("p (k n) -> p k n", k=KC)).then_inc(xT_dve, 1)

            def mask(s, gh):
                dve.wait_ge(w1_ready, G * s + 4 * gh + 4)
                nc.vector.tensor_tensor(
                    w1m[:, 4 * gh:4 * gh + 4].rearrange("p g (t b) -> p (g t) b", b=GB),
                    w1[:, 4 * gh:4 * gh + 4].rearrange("p g (t b) -> p (g t) b", b=GB),
                    batch_mask.rearrange("p (u b) -> p u b", u=1).broadcast_to([P, 4 * TS, GB]),
                    ALU.mult).then_inc(w1m_ready, 1)

            def block_of(s, gh, m):
                return slice(None), m, bass.ds(s * TS, TS), slice(4 * GB * gh, 4 * GB * (gh + 1))

            def residual(s):
                for gh in range(2):
                    for m in range(KC):
                        dve.wait_ge(attn_ready, 4 * s + 2 * gh + m + 1)
                        cols = xT[block_of(s, gh, m)]
                        nc.vector.scalar_tensor_tensor(
                            out=cols, in0=ps[:, 4 + 2 * gh + m].rearrange("p (t c) -> p t c", t=TS),
                            scalar=x_off[:, m:m + 1], in1=cols,
                            op0=ALU.add, op1=ALU.add).then_inc(x1_ready, 1)

            def rest_of_x1(grp, par, k):
                dve.wait_ge(x_hi_ready, KC * grp + k + 1)
                nc.vector.tensor_tensor(x_lo[:, par, k], x1_of(grp, k), x_hi[:, par, k].bitcast(F32),
                                        ALU.subtract).then_inc(x_lo_ready, 1)

            turned(0, 1)
            dve.wait_ge(pe_prep, 6)
            for dst, src in n_blocks(3):
                i = nc.vector.tensor_copy(dst, src)
            i.then_inc(dve_prep, 1)
            turned(0, 3)
            dve.wait_ge(u_top_ready, 1)
            nc.vector.tensor_scalar(u_pow[:].bitcast(I32), u_top[:].bitcast(I32), 0x7F800000, None,
                                    ALU.bitwise_and).then_inc(scale_ready, 1)
            dve.wait_ge(scale_ready, 1)
            nc.vector.tensor_scalar(unscale[:], u_pow[:], 2.0 ** -40, 1 / (U_TOP * H_SCALE),
                                    ALU.max, ALU.mult).then_inc(scale_ready, 1)
            dve.wait_ge(scale_ready, 2)
            nc.vector.reciprocal(scale[:], unscale[:]).then_inc(scale_ready, 1)
            dve.wait_ge(scale_ready, 3)
            nc.vector.tensor_scalar(u_scale[:], scale[:], 1 / H_SCALE, None, ALU.mult).then_inc(scale_ready, 1)
            dve.wait_ge(v_ready, 1)
            for g in range(3):
                i = nc.vector.tensor_scalar(vcond[:, g], vcond[:, g],
                                            scale[:, 0:1] if g == Z else H_SCALE, None, ALU.mult)
            i.then_inc(v_ready, 1)
            with dve.Fori(0, SLICES - 1) as s:
                for gh in range(2):
                    mask(s, gh)
                    turned(s + 1, 2 * gh + 1)
                residual(s)
            for grp in range(2):
                for k in range(KC):
                    rest_of_x1(grp, grp, k)
            for gh in range(2):
                mask(SLICES - 1, gh)
            residual(SLICES - 1)

            def in_parts(whole, a, b, op, a_ready, a_count, whole_ready, parts, parts_ready, count):
                for k in range(KC):
                    dve.wait_ge(a_ready[k], a_count)
                    if k == KC - 1:
                        nc.vector.tensor_tensor(whole, a[:], b, op).then_inc(whole_ready, 1)
                    nc.vector.tensor_tensor(parts[0][:, k], a[:, k], b[:, k], op).then_inc(parts_ready[0][k], 1)
                for k in range(KC):
                    dve.wait_ge(whole_ready if k == 0 else parts_ready[0][k], count)
                    nc.vector.tensor_tensor(parts[1][:, k], whole[:, k], parts[0][:, k],
                                            ALU.subtract).then_inc(parts_ready[1][k], 1)

            def group(grp, par, first=False, last=False):
                for v in range(GS):
                    t = GS * grp + v
                    one_more, two_more = value(dve, t + 1), value(dve, t + 2)
                    now, prev = hs[:, v % 2], hs[:, (v + 1) % 2]
                    if not (first and v == 0):
                        in_parts(rh[:], r_g, prev, ALU.mult, r_ready, one_more, rh_ready, rh16, rh16_ready, one_more)
                    if v == 0 and not (first or last):
                        rest_of_x1(grp + 1, 1 - par, 0)
                    dve.wait_ge(z_ready, one_more)
                    nc.vector.scalar_tensor_tensor(out=keep[:], in0=z_g[:], scalar=1.0, in1=prev,
                                                   op0=ALU.subtract, op1=ALU.mult)
                    for k in range(KC):
                        dve.wait_ge(c_ready[k], one_more)
                        nc.vector.scalar_tensor_tensor(out=zc[:, k], in0=z_g[:, k], scalar=H_SCALE, in1=c_g[:, k],
                                                       op0=ALU.mult, op1=ALU.mult).then_inc(zc_ready[k], 1)
                    if last and v == GS - 1:
                        for k in range(KC):
                            dve.wait_ge(zc_ready[k], one_more)
                        nc.vector.tensor_tensor(now, zc[:], keep[:], ALU.subtract).then_inc(hs_ready, 1)
                        dve.wait_ge(hs_ready, two_more)
                    else:
                        in_parts(now, zc, keep[:], ALU.subtract, zc_ready, one_more,
                                 hs_ready, h16, h16_ready, two_more)
                    slot = v // 2
                    if v % 2 == 0 and not first:
                        dve.wait_ge(yT_ready, 2 * grp + slot - 1)
                    nc.vector.scalar_tensor_tensor(
                        out=y[:, slot, :, v % 2], in0=now, scalar=1 / H_SCALE,
                        in1=xT[:, :, bass.ds(t, 1), :].rearrange("p k t b -> p k (t b)"),
                        op0=ALU.mult, op1=ALU.add).then_inc(y_ready, 1)
                    if v == 0 and not (first or last):
                        rest_of_x1(grp + 1, 1 - par, 1)

            groups(dve, group)

        @block.gpsimd
        def _(pool):
            tt, copy = nc.gpsimd.tensor_tensor, nc.gpsimd.tensor_copy
            done = [0]

            def after(i):
                i.then_inc(split, 1)
                done[0] += 1
                pool.wait_ge(split, done[0])

            pool.wait_ge(u_max_ready, 1)
            nc.gpsimd.partition_all_reduce(u_top[:], u_max[:], P, bass.bass_isa.ReduceOp.max
                                           ).then_inc(u_top_ready, 1)
            for g in (R, C, Z):
                pool.wait_ge(gate_in[g], 16 if g == Z else 16 * 2)
                if g == Z:
                    pool.wait_ge(scale_ready, 4)
                    nc.gpsimd.tensor_scalar(w_rec[g][:], w_rec[g][:], u_scale[:, 0:1], None, ALU.mult)
                after(nc.gpsimd.tensor_scalar(w_in[g][:], w_in[g][:], scale[:, 0:1] if g == Z else H_SCALE,
                                              None, ALU.mult))
                after(copy(w_hi[g][:], w_in[g][:]))
                tt(w_lo[g][:], w_in[g][:], w_hi[g][:].bitcast(F32), ALU.subtract).then_inc(w_split, 1)
                for part in u_part[g][:-1]:
                    after(copy(part[:], w_rec[g][:]))
                    if part is u_part[Z][0]:
                        tt(u_part[g][-1][:], w_rec[g][:], part[:], ALU.subtract).then_inc(w_split, 1)
                    else:
                        after(tt(w_rec[g][:], w_rec[g][:], part[:], ALU.subtract))
                if g != Z:
                    copy(u_part[g][-1][:], w_rec[g][:]).then_inc(w_split, 1)


_VECTORS = ["L0_cond_b_q", "L0_cond_no_op_k", "L0_cond_no_op_v", "L0_cond_b_kv", "L0_cond_b_proj",
            "L1_cond_b_z", "L1_cond_b_r", "L1_cond_b"]
_MATRICES = ["L0_cond_W_kv", "L0_cond_W_proj", "L1_cond_W_z", "L1_cond_U_z", "L1_cond_C_z",
             "L1_cond_W_r", "L1_cond_U_r", "L1_cond_C_r", "L1_cond_W", "L1_cond_U", "L1_cond_C"]


def kernel(**inputs):
    import numpy as np
    import concourse.bacc as bacc
    from concourse.bass_utils import run_bass_kernel_spmd

    nc = bacc.Bacc("TRN2", target_bir_lowering=False, num_devices=1)
    arrays, args = {}, []

    def give(name, a):
        a = np.ascontiguousarray(a)
        arrays[name] = a
        args.append(nc.dram_tensor(name, a.shape, mybir.dt.from_np(a.dtype), kind="ExternalInput").ap())

    x, cond = np.asarray(inputs["x"]), np.asarray(inputs["cond_1024"])
    give("in_x", x)
    blocks = [cond[:, k * P:(k + 1) * P].T for k in range(cond.shape[1] // P)]
    blocks += [np.asarray(inputs[name]).reshape(-1, P).T for name in _VECTORS]
    give("in_cond_vectors", np.concatenate(blocks, axis=1))
    p = np.arange(P)
    give("in_consts", np.concatenate([np.eye(P), p[:, None] // 16 == np.arange(HALF),
                                      p[:, None] // HALF % GB == np.arange(GB)], axis=1).astype(np.float32))
    give("in_W_qT", np.asarray(inputs["L0_cond_W_q"]).T)
    for name in _MATRICES:
        give("in_" + name, np.asarray(inputs[name]))
    args.append(nc.dram_tensor("out_0", x.shape, F32, kind="ExternalOutput").ap())
    build(nc, *args)
    r = run_bass_kernel_spmd(nc, [arrays], core_ids=[0])
    return r.results[0]["out_0"]
```
